# Optimizing a Trainium2 kernel written in Bass

```python
import numpy as np
import jax
import jax.numpy as jnp

def _softmax(x, axis=-1):
    return jax.nn.softmax(x, axis=axis)

def _gelu(x):
    return jax.nn.gelu(x, approximate=True)

def _silu(x):
    return jax.nn.silu(x)

def _sigmoid(x):
    return jax.nn.sigmoid(x)

def _layernorm(x, axis=-1, eps=1e-05):
    m = jnp.mean(x, axis=axis, keepdims=True)
    v = jnp.var(x, axis=axis, keepdims=True)
    return (x - m) / jnp.sqrt(v + eps)

def _scatter_add(tgt, idx, src, axis=0):
    return tgt.at[idx].add(src)

def _segment_sum(src, seg, n):
    return jax.ops.segment_sum(src, seg, n)
kernel_name = 'mk_recurrent_d1_jaxref_r4_9406a7'

def setup_inputs(seed: int=0):
    np.random.seed(seed)
    _w = jnp.asarray

    def _L0_attn_setup():
        import jax, jax.numpy as jnp
        import numpy as np
        import math
        EMBED_DIM = 256
        NUM_HEADS = 16
        HEAD_DIM = EMBED_DIM // NUM_HEADS
        key = jax.random.key(seed)
        ks = jax.random.split(key, 5)
        B, S, D = (2, 512, EMBED_DIM)
        s = 1.0 / math.sqrt(D)
        x = jax.random.normal(ks[0], (B, S, D), dtype=jnp.float32)
        W_qkv = jax.random.normal(ks[1], (3 * D, D), dtype=jnp.float32) * s
        b_qkv = jax.random.normal(ks[2], (3 * D,), dtype=jnp.float32) * 0.01
        W_out = jax.random.normal(ks[3], (D, D), dtype=jnp.float32) * s
        b_out = jax.random.normal(ks[4], (D,), dtype=jnp.float32) * 0.01
        return {'x': x, 'W_qkv': W_qkv, 'b_qkv': b_qkv, 'W_out': W_out, 'b_out': b_out}
    _L0_attn_in = _L0_attn_setup()

    def _L0_ffn_setup():
        import jax, jax.numpy as jnp
        import numpy as np
        B, S, H = (2, 1024, 256)
        I = 128
        E = 8
        TOPK = 2
        NGROUP = 2
        TOPK_GROUP = 1
        ROUTED_SCALE = 1.0

        def _silu(x):
            return x * jax.nn.sigmoid(x)
        key = jax.random.key(seed)
        ks = jax.random.split(key, 9)

        def w(k, shape, s=0.05):
            return jax.random.normal(k, shape, dtype=jnp.float32) * s
        return {'hidden_states': jax.random.normal(ks[0], (B, S, H), dtype=jnp.float32), 'router_weight': w(ks[1], (E, H)), 'correction_bias': w(ks[2], (E,)), 'w_gate': w(ks[3], (E, H, I)), 'w_up': w(ks[4], (E, H, I)), 'w_down': w(ks[5], (E, I, H)), 'sw_gate': w(ks[6], (H, I)), 'sw_up': w(ks[7], (H, I)), 'sw_down': w(ks[8], (I, H))}
    _L0_ffn_in = _L0_ffn_setup()
    _d = {'L0_attn_x': _L0_attn_in['x'], 'L0_attn_W_qkv': _L0_attn_in['W_qkv'], 'L0_attn_b_qkv': _L0_attn_in['b_qkv'], 'L0_attn_W_out': _L0_attn_in['W_out'], 'L0_attn_b_out': _L0_attn_in['b_out'], 'L0_ffn_router_weight': _L0_ffn_in['router_weight'], 'L0_ffn_correction_bias': _L0_ffn_in['correction_bias'], 'L0_ffn_w_gate': _L0_ffn_in['w_gate'], 'L0_ffn_w_up': _L0_ffn_in['w_up'], 'L0_ffn_w_down': _L0_ffn_in['w_down'], 'L0_ffn_sw_gate': _L0_ffn_in['sw_gate'], 'L0_ffn_sw_up': _L0_ffn_in['sw_up'], 'L0_ffn_sw_down': _L0_ffn_in['sw_down']}
    _x0 = _d['L0_attn_x']
    _d['L0_attn_x'] = jax.random.normal(jax.random.fold_in(jax.random.key(seed), 1), (4, 2048, 256), dtype=_x0.dtype)
    del _x0
    return _d

def reference(L0_attn_x, L0_attn_W_qkv, L0_attn_b_qkv, L0_attn_W_out, L0_attn_b_out, L0_ffn_router_weight, L0_ffn_correction_bias, L0_ffn_w_gate, L0_ffn_w_up, L0_ffn_w_down, L0_ffn_sw_gate, L0_ffn_sw_up, L0_ffn_sw_down):

    def _L0_attn_ref(x, W_qkv, b_qkv, W_out, b_out):
        import jax, jax.numpy as jnp
        import numpy as np
        import math
        EMBED_DIM = 256
        NUM_HEADS = 16
        HEAD_DIM = EMBED_DIM // NUM_HEADS
        B, S, D = x.shape
        H, Hd = (NUM_HEADS, HEAD_DIM)
        slopes = jnp.power(2.0, 8.0 * jnp.arange(0, -H, -1, dtype=jnp.float32) / H)
        qkv = x @ W_qkv.T + b_qkv
        qkv = qkv.reshape(B, S, 3, H, Hd).transpose(2, 0, 3, 1, 4)
        q, k, v = (qkv[0], qkv[1], qkv[2])
        scores = jnp.einsum('bhqd,bhkd->bhqk', q, k) / math.sqrt(Hd)
        pos = jnp.arange(S)
        rel = jnp.abs(pos[None, :] - pos[:, None]).astype(jnp.float32)
        bias = -slopes[:, None, None] * rel
        probs = jax.nn.softmax(scores + bias[None], axis=-1)
        out = jnp.einsum('bhqk,bhkd->bhqd', probs, v)
        out = out.transpose(0, 2, 1, 3).reshape(B, S, D)
        return out @ W_out.T + b_out

    def _L0_ffn_ref(hidden_states, router_weight, correction_bias, w_gate, w_up, w_down, sw_gate, sw_up, sw_down):
        import jax, jax.numpy as jnp
        import numpy as np
        B, S, H = (2, 1024, 256)
        I = 128
        E = 8
        TOPK = 2
        NGROUP = 2
        TOPK_GROUP = 1
        ROUTED_SCALE = 1.0

        def _silu(x):
            return x * jax.nn.sigmoid(x)
        b, s, h = hidden_states.shape
        x = hidden_states.reshape(-1, h)
        logits = x @ router_weight.T
        scores = jax.nn.sigmoid(logits)
        scores_for_choice = scores + correction_bias[None, :]
        e_per_g = E // NGROUP
        group_scores = jax.lax.top_k(scores_for_choice.reshape(-1, NGROUP, e_per_g), 2)[0].sum(-1)
        group_idx = jax.lax.top_k(group_scores, TOPK_GROUP)[1]
        group_mask = jax.nn.one_hot(group_idx, NGROUP, dtype=scores.dtype).sum(1)
        score_mask = jnp.repeat(group_mask, e_per_g, axis=1)
        masked = jnp.where(score_mask > 0, scores_for_choice, 0.0)
        topk_idx = jax.lax.top_k(masked, TOPK)[1]
        topk_w = jnp.take_along_axis(scores, topk_idx, axis=1)
        topk_w = topk_w / (topk_w.sum(-1, keepdims=True) + 1e-20)
        topk_w = topk_w * ROUTED_SCALE
        comb = (jax.nn.one_hot(topk_idx, E, dtype=x.dtype) * topk_w[..., None]).sum(1)
        g = jnp.einsum('th,ehi->tei', x, w_gate)
        u = jnp.einsum('th,ehi->tei', x, w_up)
        y = jnp.einsum('tei,eih->teh', _silu(g) * u, w_down)
        routed = jnp.einsum('teh,te->th', y, comb).reshape(b, s, h)
        shared = _silu(hidden_states @ sw_gate) * (hidden_states @ sw_up) @ sw_down
        return routed + shared
    x = L0_attn_x
    xn = _layernorm(x, axis=-1)
    s = _L0_attn_ref(xn, L0_attn_W_qkv, L0_attn_b_qkv, L0_attn_W_out, L0_attn_b_out)
    g = _silu(_L0_ffn_ref(xn, L0_ffn_router_weight, L0_ffn_correction_bias, L0_ffn_w_gate, L0_ffn_w_up, L0_ffn_w_down, L0_ffn_sw_gate, L0_ffn_sw_up, L0_ffn_sw_down))
    x = x + s * g
    return x

_drawn_inputs = setup_inputs


def setup_inputs(seed=0):
    import zlib

    import numpy as np

    out = dict(_drawn_inputs(seed))
    spreads = {}
    factors = {'L0_attn_b_qkv': 35.608,
     'L0_attn_b_out': 44.359,
     'L0_ffn_correction_bias': 14.972,
     'L0_ffn_router_weight': 3.602}
    for name, (base, spread) in spreads.items():
        noise = np.random.default_rng([zlib.crc32(name.encode()), seed]).standard_normal(out[name].shape)
        drawn = base * np.exp(spread * noise) if base else spread * noise
        out[name] = jnp.asarray(drawn.astype(out[name].dtype))
    for name, factor in factors.items():
        out[name] = (out[name] * factor).astype(out[name].dtype)
    return out
```

```python
from contextlib import ExitStack

import numpy as np

import concourse.bass as bass
from concourse import mybir

ALU = mybir.AluOpType
ACT = mybir.ActivationFunctionType
AX = mybir.AxisListType
RMAX = bass.bass_isa.ReduceOp.max
F32 = mybir.dt.float32
BF16 = mybir.dt.bfloat16
F16 = mybir.dt.float16
U16 = mybir.dt.uint16
I32 = mybir.dt.int32

P = 128
B, S, D = 4, 2048, 256
H, HD = 16, 16
E, I = 8, 128
NE = E + 1
BH = B * H
DC = D // P
TB = 512
NBLK = B * S // TB
BPB = S // TB
TT = TB // P
KT = S // P
PAIRS = 6
RB = 12
RC = 3
R0 = 16
ROWS = R0 + PAIRS * HD
DEPTH = 4
TILES = 2 * KT
RING = 3
XS = 2.0 ** 11
VW = 32
LIFT = 32.0
LEAST_SUM, MOST_SUM = 2.0 ** -48, 2.0 ** 100


def bf16_parts(a):
    parts, rest = [], np.asarray(a, np.float32)
    for _ in range(3):
        part = (rest.view(np.uint32) & np.uint32(0xFFFF0000)).view(np.float32)
        parts.append(part)
        rest = (rest - part).astype(np.float32)
    return parts


def constants():
    slope = np.power(np.float32(2), np.float32(8) * -np.arange(H, dtype=np.float32) / np.float32(H)).astype(np.float32)
    pos = np.arange(S, dtype=np.float32)
    hi, lo = np.floor(pos / P) * P, pos % P
    ones = np.ones(S, np.float32)
    q_rows = np.zeros((H, RB, S), np.float32)
    k_rows = np.zeros((H, R0, S), np.float32)
    for h in range(H):
        for n, part in enumerate(bf16_parts(slope[h:h + 1])):
            q_rows[h, 4 * n:4 * n + 4] = [part * ones, part * ones, hi, lo]
            k_rows[h, 4 * n:4 * n + 4] = [hi, lo, -part * ones, -part * ones]
        k_rows[h, RB:RB + RC] = 1.0
    j, k = np.arange(TB, dtype=np.float32), np.arange(P, dtype=np.float32)
    side = np.ones((ROWS, 1), np.float32)
    side[:RB] = -1.0
    head_of = np.zeros((P, DC, H), np.float32)
    for c in range(DC):
        head_of[np.arange(P), c, 8 * c + np.arange(P) // HD] = 1.0
    low = (np.arange(E)[None, :] < np.arange(E)[:, None]).astype(np.float32)
    as_bf16 = lambda a: (np.ascontiguousarray(a).view(np.uint32) >> 16).astype(np.uint16)
    return {
        "q_rows": as_bf16(q_rows).reshape(H * RB, S),
        "k_rows": as_bf16(k_rows).reshape(H * R0, S),
        "fold": (-2 * np.maximum(j[None] - k[:, None], 0)).astype(np.float32),
        "slopes": np.tile(slope[None], (P, 1)),
        "side": side,
        "head_of": head_of,
        "lower": np.tile(low.reshape(1, E, E), (P, 1, 1)),
        "ident": np.eye(P, dtype=np.float32),
    }


class Room:

    def __init__(self, nc, ctx, tag, keep):
        self.nc, self.ctx, self.tag, self.whole = nc, ctx, tag, keep["whole"]

    def sb(self, name, shape, dt=F32):
        return self.ctx.enter_context(self.nc.sbuf_tensor(f"{name}_{self.tag}", shape, dt))

    def ps(self, name, shape, dt=F32):
        return self.ctx.enter_context(self.nc.psum_tensor(f"{name}_{self.tag}", shape, dt))

    def sem(self, name):
        return self.whole.enter_context(self.nc.semaphore(f"{name}_{self.tag}"))


class Steps:

    def __init__(self, engine, sem, per):
        self.engine, self.sem, self.per = engine, sem, per

    def begin(self, turn):
        self.turn, self.k = turn, 0

    def __call__(self, ins):
        self.k += 1
        ins.then_inc(self.sem, 1)
        self.engine.wait_ge(self.sem, self.turn * self.per + self.k)

    def end(self):
        assert self.k == self.per, (self.k, self.per)


def tokens_stage(nc, a, keep):
    v_all, gate_all = keep["v_all"], keep["gate_all"]
    with ExitStack() as ctx:
        r = Room(nc, ctx, "tok", keep)
        ident = r.sb("ident", [P, P])
        head_of = r.sb("head_of", [P, DC, H])
        lower = r.sb("lower", [P, E, E])
        w_qkv = r.sb("w_qkv", [P, 2, DC, 3 * D], F16)
        w_r = r.sb("w_r", [P, 2, DC, E], F16)
        w_gu = r.sb("w_gu", [P, 2, 2, DC, NE, I], F16)
        flat = gate_all[:].rearrange("p t d -> p (t d)")
        at_gu = NBLK * TT * D // 2
        at_qkv = at_gu + 2 * DC * NE * I
        at_r = at_qkv + DC * 3 * D
        raw_gu = flat[:, at_gu:at_qkv].rearrange("p (w c e i) -> p w c e i", w=2, c=DC, e=NE)
        raw_qkv = flat[:, at_qkv:at_r].rearrange("p (c n) -> p c n", c=DC)
        raw_r = flat[:, at_r:at_r + DC * E].rearrange("p (c n) -> p c n", c=DC)
        peak = r.sb("peak", [P, 3])
        trough = r.sb("trough", [P, 3])
        power = r.sb("power", [P, 3])
        scale = r.sb("scale", [P, 3])
        undo = r.sb("undo", [P, 3])
        undo_q = r.sb("undo_q", [P, 1])
        w_d = r.sb("w_d", [P, NE, D])
        b_qk = r.sb("b_qk", [P, 2 * DC])
        b_v = r.sb("b_v", [P, D])
        b_c = r.sb("b_c", [P, E])
        x = r.sb("x", [P, TT, D])
        xT = r.sb("xT", [P, 2, DC, TB], F16)
        stats = r.sb("stats", [P, TT, 6])
        mv = r.sb("mv", [P, TT, 2])
        var = r.sb("var", [P, TT])
        std = r.sb("std", [P, TT])
        rstd = r.sb("rstd", [P, TT])
        qk = r.sb("qk", [P, 2 * DC, TB])
        rest = r.sb("rest", [P, 2, TB])
        parts = r.sb("parts", [P, 2, 3, TB], BF16)
        shift = r.sb("shift", [H, 3, TB], BF16)
        hid = r.sb("hid", [P, 2, TB])
        acc = r.sb("acc", [P, TT, D])
        score = r.sb("score", [P, TT, E])
        choice = r.sb("choice", [P, TT, E])
        pair = r.sb("pair", [P, TT * 2, 6])
        group = r.sb("group", [P, TT * 2])
        gmask = r.sb("gmask", [P, TT, 2])
        beat = r.sb("beat", [P, TT, E, E])
        tie = r.sb("tie", [P, TT, E, E])
        rank = r.sb("rank", [P, TT, E])
        comb = r.sb("comb", [P, TT, E])
        wsum = r.sb("wsum", [P, TT])
        wrec = r.sb("wrec", [P, TT])
        idle = r.sb("idle", [P, 1])

        T = r.ps("T", [P, DC, TB])
        GU = r.ps("GU", [P, 4, TB])
        Y = r.ps("Y", [P, 2, TB])

        PRODUCTS = [(c, w, x) for c in range(DC) for w, x in ((0, 0), (0, 1), (1, 0))]
        ORDER = (2, 3, 0, 1)
        SPLIT_AT = {2: 2, 3: 3}
        OWN_AT, STATS_AT, SHIFT_AT, NORM_AT = 3, 4, 5, 7
        loaded = r.sem("loaded")
        x_in = r.sem("x_in")
        var_ready = r.sem("var_ready")
        std_ready = r.sem("std_ready")
        xn_ready = r.sem("xn_ready")
        turned = r.sem("turned")
        xT_high = r.sem("xT_high")
        xT_low = r.sem("xT_low")
        raw_in = r.sem("raw_in")
        raw_gu_in = r.sem("raw_gu_in")
        peaked = r.sem("peaked")
        topped = r.sem("topped")
        scaled = r.sem("scaled")
        w_high = r.sem("w_high")
        w_low = r.sem("w_low")
        qk_mm = r.sem("qk_mm")
        v_mm = r.sem("v_mm")
        logit_mm = r.sem("logit_mm")
        own_mm = r.sem("own_mm")
        qk_out = r.sem("qk_out")
        v_out = r.sem("v_out")
        part1 = r.sem("part1")
        rest_ready = r.sem("rest_ready")
        part2 = r.sem("part2")
        part3 = r.sem("part3")
        parts_out = [r.sem(f"parts_out{n}") for n in range(2)]
        sig = r.sem("sig")
        own_ready = r.sem("own_ready")
        own_read = r.sem("own_read")
        shift_ready = r.sem("shift_ready")
        shift_out = r.sem("shift_out")
        gu_mm = r.sem("gu_mm")
        silu = r.sem("silu")
        hid_ready = r.sem("hid_ready")
        down_mm = r.sem("down_mm")
        added = r.sem("added")
        gate_out = r.sem("gate_out")
        dve_step = r.sem("dve_step")
        ln_step = r.sem("ln_step")

        wT = a["wT_qkv"].rearrange("(c p) n -> p c n", p=P)
        first_loads = [(ident[:], a["ident"]), (raw_qkv, wT), (raw_r, a["wT_router"].rearrange("(c p) n -> p c n", p=P))]
        gu_loads = []
        for c in range(DC):
            rows = slice(c * P, (c + 1) * P)
            for n, (w, sw) in enumerate((("w_gate", "sw_gate"), ("w_up", "sw_up"))):
                gu_loads += [(raw_gu[:, n, c, 0:E, :], a[w][:, rows, :].rearrange("e p i -> p e i")),
                             (raw_gu[:, n, c, E, :], a[sw][rows, :])]
        loads = [
            (b_qk[:], a["b_qkv"].rearrange("(c p) -> p c", p=P)[:, 0:2 * DC]),
            (b_v[:], a["b_qkv"].rearrange("(o n) -> o n", o=1)[:, 2 * D:3 * D].broadcast_to([P, D])),
            (b_c[:], a["correction_bias"].rearrange("(o n) -> o n", o=1).broadcast_to([P, E])),
            (head_of[:], a["head_of"]), (lower[:], a["lower"]),
            (w_d[:, 0:E, :], a["w_down"].rearrange("e i h -> i e h")),
            (w_d[:, E, :], a["sw_down"]),
        ]
        ALL_LOADED = 16 * len(loads)

        x_rows = a["x"].rearrange("b s d -> (b s) d")
        q_parts = keep["q_parts"].rearrange("(n p d) s -> n p d s", p=3, d=HD)
        k_parts = keep["k_parts"].rearrange("(n p d) s -> n p d s", p=3, d=HD)
        shifts = keep["shifts"].rearrange("(n p) s -> n p s", p=RC)

        with nc.Block() as block:
            @block.sync
            def _(sp):
                def load_x(j):
                    sp.dma_start(x[:], x_rows[bass.ds(j * TB, TB), :].rearrange("(t p) d -> p t d", p=P)).then_inc(x_in, 16)

                def store_parts(b, g):
                    j = b * BPB + g
                    for k, m in enumerate(ORDER):
                        dst = (q_parts if m < DC else k_parts)[bass.ds(b * H + 8 * (m % DC), 8), :, :, g * TB:(g + 1) * TB]
                        sp.wait_ge(part1, 4 * j + k + 1)
                        sp.wait_ge(part2, 4 * j + k + 1)
                        sp.wait_ge(part3, 4 * j + k + 1)
                        for n in range(3):
                            sp.dma_start(dst[:, n], parts[:, k % 2, n, :]).then_inc(parts_out[k % 2], 16)
                    sp.wait_ge(shift_ready, j + 1)
                    for n in range(3):
                        sp.dma_start(shifts[bass.ds(b * H, H), n, g * TB:(g + 1) * TB], shift[:, n, :]).then_inc(shift_out, 16)

                load_x(0)
                with nc.allow_non_contiguous_dma(reason="512 biases, once"):
                    for group, sem in ((first_loads, raw_in), (gu_loads, raw_gu_in), (loads, loaded)):
                        for dst, src in group:
                            sp.dma_start(dst, src).then_inc(sem, 16)
                with sp.Fori(0, B - 1) as b:
                    for g in range(BPB):
                        sp.wait_ge(turned, b * BPB + g + 1)
                        load_x(b * BPB + g + 1)
                        store_parts(b, g)
                for g in range(BPB):
                    if g < BPB - 1:
                        sp.wait_ge(turned, (B - 1) * BPB + g + 1)
                        load_x((B - 1) * BPB + g + 1)
                    store_parts(B - 1, g)
                for n in range(2):
                    sp.wait_ge(parts_out[n], 16 + 96 * NBLK)
                sp.wait_ge(shift_out, 16 + 48 * NBLK)

            @block.tensor
            def _(pe):
                def gate_up(j, e):
                    if e < 2:
                        pe.wait_ge(qk_out, 4 * j + 4 - 2 * e)
                    else:
                        pe.wait_ge(hid_ready, NE * j + e - 1)
                    for n in range(2):
                        for k, (c, w, x) in enumerate(PRODUCTS):
                            mm = pe.matmul(GU[:, 2 * (e % 2) + n, :], w_gu[:, w, n, c, e, :], xT[:, x, c, :],
                                           start=(k == 0), stop=(k == len(PRODUCTS) - 1))
                    mm.then_inc(gu_mm, 1)

                def down(j, e):
                    pe.wait_ge(hid_ready, NE * j + e + 1)
                    if e == 0:
                        pe.wait_ge(sig, j + 1)
                    else:
                        pe.wait_ge(added, NE * j + e)
                    for t in range(TT):
                        mm = pe.matmul(Y[:, t // 2, (t % 2) * D:(t % 2 + 1) * D], hid[:, e % 2, t * P:(t + 1) * P],
                                       w_d[:, e, :], start=True, stop=True)
                    mm.then_inc(down_mm, 1)

                def turn(j):
                    pe.wait_ge(xn_ready, j + 1)
                    pe.wait_ge(v_out, j + 1)
                    pe.wait_ge(own_read, j + 1)
                    for c in range(DC):
                        for t in range(TT):
                            mm = pe.transpose(T[:, c, t * P:(t + 1) * P], x[:, t, c * P:(c + 1) * P], ident[:])
                    mm.then_inc(turned, 1)

                def chunks(ms):
                    for m in ms:
                        for k, (c, w, x) in enumerate(PRODUCTS):
                            mm = pe.matmul(GU[:, m, :], w_qkv[:, w, c, m * P:(m + 1) * P], xT[:, x, c, :],
                                           start=(k == 0), stop=(k == len(PRODUCTS) - 1))
                        mm.then_inc(qk_mm, 1)

                def k_chunks(j):
                    pe.wait_ge(xT_high, 2 * j + 2)
                    pe.wait_ge(xT_low, j + 1)
                    chunks(ORDER[:2])

                def body(j, last):
                    chunks(ORDER[2:])
                    for t in range(TT):
                        for k, (c, w, x) in enumerate(PRODUCTS):
                            mm = pe.matmul(T[:, t // 2, (t % 2) * D:(t % 2 + 1) * D], xT[:, x, c, t * P:(t + 1) * P],
                                           w_qkv[:, w, c, 2 * D:3 * D], start=(k == 0), stop=(k == len(PRODUCTS) - 1))
                    mm.then_inc(v_mm, 1)
                    pe.wait_ge(gate_out, j + 1)
                    for t in range(TT):
                        for k, (c, w, x) in enumerate(PRODUCTS):
                            mm = pe.matmul(Y[:, 0, t * E:(t + 1) * E], xT[:, x, c, t * P:(t + 1) * P],
                                           w_r[:, w, c, :], start=(k == 0), stop=(k == len(PRODUCTS) - 1))
                    mm.then_inc(logit_mm, 1)
                    gate_up(j, 0)
                    for e in range(1, NE):
                        gate_up(j, e)
                        if e == NE - 1 and not last:
                            turn(j + 1)
                        down(j, e - 1)
                        if e == OWN_AT:
                            pe.wait_ge(own_ready, j + 1)
                            pe.wait_ge(v_out, j + 2)
                            for c in range(DC):
                                mm = pe.matmul(T[0:H, 0, :], head_of[:, c, :], qk[:, DC + c, :], start=(c == 0), stop=(c == DC - 1))
                            mm.then_inc(own_mm, 1)
                    if not last:
                        k_chunks(j + 1)
                    down(j, NE - 1)

                pe.wait_ge(raw_in, 16 * len(first_loads))
                turn(0)
                pe.wait_ge(w_high, 2)
                pe.wait_ge(w_low, 2)
                k_chunks(0)
                pe.wait_ge(w_high, 3)
                pe.wait_ge(w_low, 3)
                pe.wait_ge(loaded, ALL_LOADED)
                with pe.Fori(0, NBLK - 1) as j:
                    body(j, False)
                body(NBLK - 1, True)

            @block.gpsimd
            def _(pool):
                for n, (lo, hi) in enumerate(((0, 2), (2, 3))):
                    pool.wait_ge(peaked, n + 1)
                    nc.gpsimd.partition_all_reduce(power[:, lo:hi], peak[:, lo:hi], P, RMAX).then_inc(topped, 1)

            @block.scalar
            def _(act):
                def high(n, dst, src):
                    nc.scalar.activation(dst, src, ACT.Copy, scale=scale[:, n:n + 1]).then_inc(w_high, 1)

                def root():
                    return nc.scalar.activation(std[:], var[:], ACT.Sqrt)

                def split(j, k):
                    act.wait_ge(qk_out, 4 * j + k + 1)
                    act.wait_ge(parts_out[k % 2], 96 * j + 48 * (k // 2) + 16)
                    nc.scalar.copy(parts[:, k % 2, 0, :], qk[:, ORDER[k], :]).then_inc(part1, 1)
                    act.wait_ge(rest_ready, 4 * j + k + 1)
                    nc.scalar.copy(parts[:, k % 2, 1, :], rest[:, k % 2, :]).then_inc(part2, 1)

                def take_xT(j):
                    act.wait_ge(turned, j + 1)
                    for c in range(DC):
                        nc.scalar.activation(xT[:, 0, c, :], T[:, c, :], ACT.Copy, scale=XS).then_inc(xT_high, 1)

                def body(j, last):
                    for k in range(2):
                        split(j, k)
                    act.wait_ge(logit_mm, j + 1)
                    nc.scalar.activation(score[:].rearrange("p t e -> p (t e)"), Y[:, 0, 0:TT * E], ACT.Sigmoid,
                                         scale=undo[:, 1:2]).then_inc(sig, 1)
                    for e in range(NE):
                        act.wait_ge(gu_mm, NE * j + e + 1)
                        act.wait_ge(down_mm, NE * j + max(e - 1, 0) + 1)
                        nc.scalar.activation(hid[:, e % 2, :], GU[:, 2 * (e % 2), :], ACT.Silu,
                                             scale=undo[:, 2:3]).then_inc(silu, 1)
                        if e in SPLIT_AT:
                            split(j, SPLIT_AT[e])
                        if e == STATS_AT + 1 and not last:
                            act.wait_ge(var_ready, j + 2)
                            root().then_inc(std_ready, 1)
                    if not last:
                        take_xT(j + 1)
                    act.wait_ge(added, NE * (j + 1))
                    nc.scalar.activation(gate_all[:, bass.ds(j * TT, TT), :], acc[:], ACT.Silu).then_inc(gate_out, 1)

                act.sem_inc(parts_out[0], 16)
                act.sem_inc(parts_out[1], 16)
                act.sem_inc(down_mm, 1)
                act.wait_ge(var_ready, 1)
                root().then_inc(std_ready, 1)
                act.wait_ge(scaled, 1)
                high(0, w_qkv[:, 0], raw_qkv)
                high(1, w_r[:, 0], raw_r)
                take_xT(0)
                act.wait_ge(scaled, 2)
                high(2, w_gu[:, 0].rearrange("p w c e i -> p (w c e i)"), flat[:, at_gu:at_qkv])
                with act.Fori(0, NBLK - 1) as j:
                    body(j, False)
                body(NBLK - 1, True)

            @block.vector
            def _(dve):
                v = nc.vector
                step = Steps(dve, dve_step, 17)
                ln = Steps(dve, ln_step, 3)

                once = Steps(dve, r.sem("dve_once"), 11)
                once.begin(0)

                def peaks(n, raw, axes):
                    v.tensor_reduce(peak[:, n:n + 1], raw, axes, ALU.max)
                    return v.tensor_reduce(trough[:, n:n + 1], raw, axes, ALU.min)

                def top(lo, hi):
                    v.scalar_tensor_tensor(out=peak[:, lo:hi], in0=trough[:, lo:hi], scalar=-1.0, in1=peak[:, lo:hi],
                                           op0=ALU.mult, op1=ALU.max).then_inc(peaked, 1)

                def scales(lo, hi, n):
                    dve.wait_ge(topped, n + 1)
                    top, mask = power[:, lo:hi], 0x7F800000
                    once(v.tensor_scalar(top, top, 2.0 ** -96, None, ALU.max))
                    once(v.tensor_scalar(top.bitcast(I32), top.bitcast(I32), mask, None, ALU.bitwise_and))
                    v.tensor_scalar(undo[:, lo:hi], top, 2.0 ** -14 / XS, None, ALU.mult)
                    once(v.reciprocal(scale[:, lo:hi], top))
                    once(v.tensor_scalar(scale[:, lo:hi], scale[:, lo:hi], 2.0 ** 14, None, ALU.mult))
                    v.tensor_scalar(undo_q[:], undo[:, 0:1], HD ** -0.5, None, ALU.mult).then_inc(scaled, 1)

                def low(n, w, raw):
                    dve.wait_ge(w_high, n + 1)
                    v.scalar_tensor_tensor(out=w[:, 1], in0=raw, scalar=scale[:, n:n + 1], in1=w[:, 0],
                                           op0=ALU.mult, op1=ALU.subtract).then_inc(w_low, 1)

                def ln_stats(j):
                    ln.begin(j)
                    dve.wait_ge(x_in, 16 * (j + 1))
                    for t in range(TT):
                        last = v.bn_stats(stats[:, t, :], x[:, t, :])
                    ln(last)
                    v.memset(idle[:], 0.0)
                    for t in range(TT):
                        last = v.bn_aggr(mv[:, t, :], stats[:, t, :])
                    ln(last)
                    v.tensor_scalar(var[:], mv[:, :, 1], 1e-5, None, ALU.add).then_inc(var_ready, 1)

                def ln_apply(j):
                    dve.wait_ge(std_ready, j + 1)
                    ln(v.reciprocal(rstd[:], std[:]))
                    for t in range(TT):
                        ins = v.tensor_scalar(x[:, t, :], x[:, t, :], mv[:, t, 0:1], rstd[:, t:t + 1], ALU.subtract, ALU.mult)
                    ins.then_inc(xn_ready, 1)
                    ln.end()

                def rivals(j):
                    dve.wait_ge(sig, j + 1)
                    step(v.tensor_tensor(choice[:], score[:], b_c[:].unsqueeze(1).broadcast_to([P, TT, E]), ALU.add))
                    c4 = choice[:].rearrange("p t (g k) -> p (t g) k", g=2)
                    v.tensor_tensor(pair[:, :, 0:3], c4[:, :, 0:3], c4[:, :, 1:4], ALU.add)
                    v.tensor_tensor(pair[:, :, 3:5], c4[:, :, 0:2], c4[:, :, 2:4], ALU.add)
                    step(v.tensor_tensor(pair[:, :, 5:6], c4[:, :, 0:1], c4[:, :, 3:4], ALU.add))
                    step(v.tensor_reduce(group[:], pair[:], AX.X, ALU.max))
                    g2 = group[:].rearrange("p (t g) -> p t g", g=2)
                    v.tensor_tensor(gmask[:, :, 0:1], g2[:, :, 0:1], g2[:, :, 1:2], ALU.is_ge)
                    step(v.tensor_tensor(gmask[:, :, 1:2], g2[:, :, 0:1], g2[:, :, 1:2], ALU.is_lt))
                    for g in range(2):
                        ins = v.tensor_tensor(choice[:, :, 4 * g:4 * g + 4], choice[:, :, 4 * g:4 * g + 4],
                                              gmask[:, :, g:g + 1].broadcast_to([P, TT, 4]), ALU.mult)
                    step(ins)
                    me = choice[:].unsqueeze(3).broadcast_to([P, TT, E, E])
                    other = choice[:].unsqueeze(2).broadcast_to([P, TT, E, E])
                    v.tensor_tensor(beat[:], other, me, ALU.is_gt)
                    step(v.tensor_tensor(tie[:], other, me, ALU.is_equal))

                def weights(j):
                    step(v.tensor_tensor(tie[:], tie[:], lower[:].unsqueeze(1).broadcast_to([P, TT, E, E]), ALU.mult))
                    step(v.tensor_tensor(beat[:], beat[:], tie[:], ALU.add))
                    step(v.tensor_reduce(rank[:], beat[:], AX.X, ALU.add))
                    step(v.scalar_tensor_tensor(out=comb[:], in0=rank[:], scalar=1.5, in1=score[:], op0=ALU.is_lt, op1=ALU.mult))
                    step(v.tensor_reduce(wsum[:], comb[:], AX.X, ALU.add))
                    step(v.tensor_scalar(wsum[:], wsum[:], 1e-20, None, ALU.add))
                    step(v.reciprocal(wrec[:], wsum[:]))
                    step(v.tensor_tensor(comb[:], comb[:], wrec[:].unsqueeze(2).broadcast_to([P, TT, E]), ALU.mult))

                def weigh(j, e):
                    dve.wait_ge(down_mm, NE * j + e + 1 + 1)
                    if e == 0:
                        dve.wait_ge(gate_out, j + 1)
                    for t in range(TT):
                        y = Y[:, t // 2, (t % 2) * D:(t % 2 + 1) * D]
                        if e == 0:
                            ins = v.tensor_scalar(acc[:, t, :], y, comb[:, t, 0:1], None, ALU.mult)
                        elif e < E:
                            ins = v.scalar_tensor_tensor(out=acc[:, t, :], in0=y, scalar=comb[:, t, e:e + 1],
                                                         in1=acc[:, t, :], op0=ALU.mult, op1=ALU.add)
                        else:
                            ins = v.tensor_tensor(acc[:, t, :], y, acc[:, t, :], ALU.add)
                    ins.then_inc(added, 1)
                    dve.wait_ge(added, NE * j + e + 1)

                def shifts_of(j):
                    own = qk[0:H, DC, :]
                    dve.wait_ge(own_mm, j + 2)
                    v.tensor_scalar(own, T[0:H, 0, :], -1.0, -LIFT, ALU.mult, ALU.add).then_inc(own_read, 1)
                    dve.wait_ge(own_read, j + 2)
                    dve.wait_ge(shift_out, 48 * j + 16)
                    step(v.tensor_copy(shift[:, 0, :], own))
                    step(v.tensor_tensor(own, own, shift[:, 0, :], ALU.subtract))
                    step(v.tensor_copy(shift[:, 1, :], own))
                    v.tensor_tensor(shift[:, 2, :], own, shift[:, 1, :], ALU.subtract).then_inc(shift_ready, 1)

                def split(j, k):
                    m = ORDER[k]
                    dve.wait_ge(part1, 4 * j + k + 1)
                    dve.wait_ge(qk_out, 4 * j + k + 1)
                    v.tensor_tensor(rest[:, k % 2, :], qk[:, m, :], parts[:, k % 2, 0, :], ALU.subtract).then_inc(rest_ready, 1)
                    dve.wait_ge(part2, 4 * j + k + 1)
                    dve.wait_ge(rest_ready, 4 * j + k + 1)
                    v.tensor_tensor(parts[:, k % 2, 2, :], rest[:, k % 2, :], parts[:, k % 2, 1, :], ALU.subtract).then_inc(part3, 1)

                def take_xT(j):
                    for c in range(DC):
                        dve.wait_ge(xT_high, 2 * j + c + 1)
                        ins = v.scalar_tensor_tensor(out=xT[:, 1, c, :], in0=T[:, c, :], scalar=XS, in1=xT[:, 0, c, :],
                                                     op0=ALU.mult, op1=ALU.subtract)
                    ins.then_inc(xT_low, 1)

                def body(j, last):
                    step.begin(j)
                    for k, m in enumerate(ORDER):
                        dve.wait_ge(qk_mm, 4 * j + k + 1)
                        if k == 0:
                            dve.wait_ge(own_mm, j + 1)
                        v.tensor_scalar(qk[:, m, :], GU[:, m, :], undo_q[:] if m < DC else undo[:, 0:1], b_qk[:, m:m + 1],
                                        ALU.mult, ALU.add).then_inc(qk_out, 1)
                    split(j, 0)
                    dve.wait_ge(v_mm, j + 1)
                    v.scalar_tensor_tensor(out=v_all[:, bass.ds(j * TT, TT), :], in0=T[:].rearrange("p a (b d) -> p (a b) d", d=D),
                                           scalar=undo[:, 0:1], in1=b_v[:].unsqueeze(1).broadcast_to([P, TT, D]),
                                           op0=ALU.mult, op1=ALU.add).then_inc(v_out, 1)
                    split(j, 1)
                    for e in range(NE):
                        dve.wait_ge(silu, NE * j + e + 1)
                        v.scalar_tensor_tensor(out=hid[:, e % 2, :], in0=GU[:, 2 * (e % 2) + 1, :], scalar=undo[:, 2:3],
                                               in1=hid[:, e % 2, :], op0=ALU.mult, op1=ALU.mult).then_inc(hid_ready, 1)
                        if e == 0:
                            rivals(j)
                        if e == 1:
                            weights(j)
                            weigh(j, 0)
                            for c in range(DC):
                                ins = v.tensor_tensor(qk[:, DC + c, :], qk[:, c, :], qk[:, DC + c, :], ALU.mult)
                            ins.then_inc(own_ready, 1)
                        if e == STATS_AT and not last:
                            ln_stats(j + 1)
                        if e == NORM_AT and not last:
                            ln_apply(j + 1)
                        if e == NE - 1 and not last:
                            take_xT(j + 1)
                        if e > 1:
                            weigh(j, e - 1)
                        if e in SPLIT_AT:
                            split(j, SPLIT_AT[e])
                        if e == SHIFT_AT:
                            shifts_of(j)
                    weigh(j, NE - 1)
                    step.end()

                dve.sem_inc(v_out, 1)
                dve.sem_inc(gate_out, 1)
                dve.sem_inc(own_mm, 1)
                dve.sem_inc(own_read, 1)
                dve.sem_inc(shift_out, 16)
                ln_stats(0)
                ln_apply(0)
                dve.wait_ge(raw_in, 16 * len(first_loads))
                peaks(0, raw_qkv, AX.XY)
                once(peaks(1, raw_r, AX.XY))
                top(0, 2)
                scales(0, 2, 0)
                low(0, w_qkv, raw_qkv)
                low(1, w_r, raw_r)
                take_xT(0)
                dve.wait_ge(raw_gu_in, 16 * len(gu_loads))
                once(peaks(2, flat[:, at_gu:at_qkv], AX.X))
                top(2, 3)
                scales(2, 3, 1)
                dve.wait_ge(w_high, 3)
                v.scalar_tensor_tensor(out=w_gu[:, 1].rearrange("p w c e i -> p (w c e i)"), in0=flat[:, at_gu:at_qkv],
                                       scalar=scale[:, 2:3], in1=w_gu[:, 0].rearrange("p w c e i -> p (w c e i)"),
                                       op0=ALU.mult, op1=ALU.subtract).then_inc(w_low, 1)
                dve.wait_ge(loaded, ALL_LOADED)
                once(v.tensor_scalar(b_qk[:, 0:DC], b_qk[:, 0:DC], HD ** -0.5, None, ALU.mult))
                once.end()
                with dve.Fori(0, NBLK - 1) as j:
                    body(j, False)
                body(NBLK - 1, True)


def load_stacks(engine, a, keep, n, Q, K, sem, shifted=True):
    q, k = keep["q_parts"], keep["k_parts"]
    first, head = n * (3 * HD), n % H
    engine.dma_start(Q[0:RB, :].bitcast(U16), a["q_rows"][bass.ds(head * RB, RB), :]).then_inc(sem, 16)
    engine.dma_start(K[0:R0, :].bitcast(U16), a["k_rows"][bass.ds(head * R0, R0), :]).then_inc(sem, 16)
    if shifted:
        engine.dma_start(Q[RB:RB + RC, :], keep["shifts"][bass.ds(n * RC, RC), :]).then_inc(sem, 16)
    at = R0
    for part in range(3):
        rows = (3 - part) * HD
        engine.dma_start(Q[at:at + rows, :], q[bass.ds(first, rows), :]).then_inc(sem, 16)
        same = k[bass.ds(first + part * HD, HD), :].unsqueeze(0).broadcast_to([3 - part, HD, S])
        engine.dma_start(K[at:at + rows, :], same).then_inc(sem, 16)
        at += rows


LOADS = 16 * 9


def attention_stage(nc, a, keep, tag):
    v_all = keep["v_all"]
    with ExitStack() as ctx:
        r = Room(nc, ctx, tag, keep)
        Q = [r.sb(f"Q{n}", [ROWS, S], BF16) for n in range(2)]
        K = [[r.sb(f"K{n}{s}", [ROWS, S], BF16) for s in range(2)] for n in range(2)]
        V = [r.sb(f"V{n}", [P, KT, VW]) for n in range(2)]
        probs = [r.sb(f"probs{n}", [P, S]) for n in range(DEPTH)]
        out = [r.sb(f"out{n}", [P, TB]) for n in range(2)]
        fold = r.sb("fold", [P, TB])
        slopes = r.sb("slopes", [P, H])
        side = r.sb("side", [ROWS, 1])
        SC = r.ps("SC", [P, RING, 2, TB])
        O = r.ps("O", [P, 2, TB])

        loaded = r.sem("loaded")
        zeroed = r.sem("zeroed")
        stacks_in = [r.sem(f"stacks_in{n}") for n in range(2)]
        k_turned = r.sem("k_turned")
        v_in = r.sem("v_in")
        scored = r.sem("scored")
        folded = r.sem("folded")
        expd = r.sem("expd")
        pv = r.sem("pv")
        o_read = r.sem("o_read")
        o_out = [r.sem(f"o_out{n}") for n in range(2)]

        with nc.Block() as block:
            @block.sync
            def _(sp):
                for dst, src in ((fold[:], a["fold"]), (slopes[:], a["slopes"]), (side[:], a["side"])):
                    sp.dma_start(dst, src).then_inc(loaded, 16)
                sp.wait_ge(zeroed, 1)

                def store(n, par):
                    sp.wait_ge(o_read, n + 1 + 2)
                    sp.dma_start(keep["sums"][bass.ds(n * P, P), :], out[par][:]).then_inc(o_out[par], 16)

                for par in range(2):
                    load_stacks(sp, a, keep, par, Q[par], K[par][0], stacks_in[par])
                with sp.Fori(0, BH // 2 - 1) as i:
                    for par in range(2):
                        sp.wait_ge(scored, TILES * (2 * i + par + 1))
                        load_stacks(sp, a, keep, 2 * i + par + 2, Q[par], K[par][0], stacks_in[par])
                        store(2 * i + par, par)
                for par in range(2):
                    store(BH - 2 + par, par)
                for par in range(2):
                    sp.wait_ge(o_out[par], 16 * (BH // 2 + 1))

            @block.gpsimd
            def _(pool):
                def stage_v(n, par):
                    src = v_all[:, bass.ds(n // H * KT, KT), bass.ds(n % H * HD, HD)]
                    nc.gpsimd.tensor_copy(V[par][:, :, 0:HD], src).then_inc(v_in, 1)

                for n in range(2):
                    nc.gpsimd.memset(Q[n][:], 0.0)
                nc.gpsimd.drain().then_inc(zeroed, 1)
                for n in range(2):
                    nc.gpsimd.memset(V[n][:], 0.0)
                nc.gpsimd.drain().then_inc(zeroed, 1)
                pool.wait_ge(zeroed, 2)
                for n in range(2):
                    nc.gpsimd.memset(V[n][:, :, HD:HD + 1], 1.0).then_inc(zeroed, 1)
                for par in range(2):
                    stage_v(par, par)
                with pool.Fori(1, BH // 2) as i:
                    for par in range(2):
                        pool.wait_ge(pv, KT * (2 * i + par - 1) + DEPTH)
                        stage_v(2 * i + par, par)

            @block.tensor
            def _(pe):
                def scores(n, turn, par, t):
                    kt, half = t // 2, t % 2
                    if t == 0:
                        pe.wait_ge(stacks_in[par], LOADS * (turn + 1))
                        pe.wait_ge(k_turned, n + 1)
                    before = {0: -2, 1: -1, 2: -3}.get(t, t - RING)
                    pe.wait_ge(expd, TILES * n + before + 1 + RING)
                    for x in range(2):
                        bank = 2 * half + x
                        stack = K[par][0 if bank > kt // TT else 1]
                        mm = pe.matmul(SC[:, t % RING, x, :], stack[:, kt * P:(kt + 1) * P],
                                       Q[par][:, bank * TB:(bank + 1) * TB], start=True, stop=True)
                    mm.then_inc(scored, 1)

                def weighted_sum(n, par, kt):
                    if kt == 0:
                        pe.wait_ge(v_in, n + 1)
                        pe.wait_ge(o_read, n + 1)
                    pe.wait_ge(expd, TILES * n + 2 * kt + 2 + RING)
                    for g in range(BPB):
                        mm = pe.matmul(O[VW * g:VW * (g + 1), par, :], V[par][:, kt, :],
                                       probs[kt % DEPTH][:, g * TB:(g + 1) * TB], start=(kt == 0), stop=(kt == KT - 1))
                    mm.then_inc(pv, 1)

                def body(i, last):
                    for par in range(2):
                        n = 2 * i + par
                        for kt in range(KT):
                            for t in (2 * kt + 4, 2 * kt + 5):
                                if t < TILES:
                                    scores(n, i, par, t)
                                elif par == 0:
                                    scores(n + 1, i, 1, t - TILES)
                                elif not last:
                                    scores(n + 1, i + 1, 0, t - TILES)
                            weighted_sum(n, par, kt)

                pe.wait_ge(zeroed, 4)
                for t in range(4):
                    scores(0, 0, 0, t)
                with pe.Fori(0, BH // 2 - 1) as i:
                    body(i, False)
                body(BH // 2 - 1, True)

            @block.scalar
            def _(act):
                act.sem_inc(expd, RING)
                act.sem_inc(pv, DEPTH)
                act.sem_inc(o_read, 2)
                with act.Fori(0, BH // 2) as i:
                    for par in range(2):
                        n = 2 * i + par
                        for t in range(TILES):
                            kt, half = t // 2, t % 2
                            if half == kt // TT // 2:
                                act.wait_ge(folded, KT * n + kt + 1)
                            else:
                                act.wait_ge(scored, TILES * n + t + 1)
                            if half == 0:
                                act.wait_ge(pv, KT * n + kt + 1)
                            nc.scalar.activation(probs[kt % DEPTH][:, half * 2 * TB:(half + 1) * 2 * TB],
                                                 SC[:, t % RING].rearrange("p a b -> p (a b)"), ACT.Exp).then_inc(expd, 1)

            @block.vector
            def _(dve):
                v = nc.vector

                def turn_k(n, turn, par):
                    dve.wait_ge(stacks_in[par], LOADS * (turn + 1))
                    v.tensor_scalar(K[par][1][:], K[par][0][:], side[:], None, ALU.mult).then_inc(k_turned, 1)

                def fold_bias(n, kt):
                    bank, at = kt // TT, kt % TT * P
                    t = 2 * kt + bank // 2
                    dve.wait_ge(scored, TILES * n + t + 1)
                    sc = SC[:, t % RING, bank % 2, at:TB]
                    v.scalar_tensor_tensor(out=sc, in0=fold[:, 0:TB - at], scalar=slopes[:, bass.ds(n % H, 1)],
                                           in1=sc, op0=ALU.mult, op1=ALU.add).then_inc(folded, 1)

                def read_out(n, turn, par):
                    dve.wait_ge(pv, KT * (n + 1) + DEPTH)
                    dve.wait_ge(o_out[par], 16 * turn + 16)
                    v.tensor_copy(out[par][:], O[:, par, :]).then_inc(o_read, 1)

                def body(i, last):
                    for par in range(2):
                        n, more = 2 * i + par, par == 0 or not last
                        for kt in range(2, KT):
                            fold_bias(n, kt)
                            if kt == KT // 2 and more:
                                turn_k(n + 1, i + par, 1 - par)
                        if more:
                            fold_bias(n + 1, 0)
                            fold_bias(n + 1, 1)
                        read_out(n, i, par)

                for par in range(2):
                    dve.sem_inc(o_out[par], 16)
                dve.wait_ge(loaded, 48)
                turn_k(0, 0, 0)
                fold_bias(0, 0)
                fold_bias(0, 1)
                with dve.Fori(0, BH // 2 - 1) as i:
                    body(i, False)
                body(BH // 2 - 1, True)


def sums_stage(nc, keep, tag):
    redo = keep["redo"]
    with ExitStack() as ctx:
        r = Room(nc, ctx, tag, keep)
        sums = r.sb("sums", [P, 2, TB])
        fine = r.sb("fine", [P, 2, TB])
        low = r.sb("low", [P, 2, TB])
        all_fine = r.sb("all_fine", [P, 1])
        ones = r.sb("ones", [P, 1])
        count = r.ps("count", [P, TB])
        sums_in, out, step, counted = r.sem("sums_in"), r.sem("out"), r.sem("step"), r.sem("counted")
        rows = keep["sums"].rearrange("(p t r) q -> p t r q", t=2, r=VW)[:, :, HD, :]
        with nc.Block() as block:
            @block.sync
            def _(sp):
                sp.dma_start(sums[:], rows).then_inc(sums_in, 16)
                sp.wait_ge(step, 1)
                sp.dma_start(keep["recips"].rearrange("(p t) q -> p t q", t=2), low[:]).then_inc(out, 16)
                sp.wait_ge(out, 16)

            @block.vector
            def _(dve):
                v = nc.vector
                steps = Steps(dve, step, 6)
                steps.begin(0)
                dve.wait_ge(sums_in, 16)
                steps(v.reciprocal(low[:], sums[:]))
                v.memset(ones[:], 1.0)
                steps(v.tensor_scalar(fine[:], sums[:], MOST_SUM, None, ALU.is_le))
                steps(v.tensor_scalar(sums[:], sums[:], LEAST_SUM, None, ALU.is_ge))
                steps(v.tensor_tensor(fine[:], fine[:], sums[:], ALU.mult))
                steps(v.tensor_reduce(all_fine[:], fine[:], AX.XY, ALU.min))
                dve.wait_ge(counted, 1)
                steps(v.tensor_scalar(redo[0:1, :], count[0:1, 0:1], P - 0.5, None, ALU.is_lt))
                steps.end()

            @block.tensor
            def _(pe):
                pe.wait_ge(step, 5)
                pe.matmul(count[0:1, 0:1], all_fine[:], ones[:], start=True, stop=True).then_inc(counted, 1)


def maximum_stage(nc, a, keep):
    with ExitStack() as ctx:
        r = Room(nc, ctx, "max", keep)
        Q = r.sb("Q", [ROWS, S], BF16)
        K = [r.sb(f"K{s}", [ROWS, S], BF16) for s in range(2)]
        fold = r.sb("fold", [P, TB])
        slopes = r.sb("slopes", [P, H])
        side = r.sb("side", [ROWS, 1])
        ident = r.sb("ident", [P, P])
        top = r.sb("top", [P, KT])
        neg = r.sb("neg", [KT, P])
        parts = r.sb("parts", [KT, RC, P], BF16)
        SC = r.ps("SC", [P, BPB, TB])
        T = r.ps("T", [P, TB])
        loaded, zeroed, stacks_in, k_turned = r.sem("loaded"), r.sem("zeroed"), r.sem("stacks_in"), r.sem("k_turned")
        scored, topped, turned, shift_out, step = (r.sem("scored"), r.sem("topped"), r.sem("turned"),
                                                   r.sem("shift_out"), r.sem("step"))
        PER = KT + 5
        shifts = keep["shifts"].rearrange("(n p) (t q) -> n p t q", p=RC, q=P)
        with nc.Block() as block:
            @block.gpsimd
            def _(pool):
                nc.gpsimd.memset(Q[:], 0.0).then_inc(zeroed, 1)

            @block.scalar
            def _(act):
                for dst, src in ((fold[:], a["fold"]), (slopes[:], a["slopes"]), (side[:], a["side"]), (ident[:], a["ident"])):
                    act.dma_start(dst, src).then_inc(loaded, 16)

            @block.sync
            def _(sp):
                sp.wait_ge(zeroed, 1)
                load_stacks(sp, a, keep, 0, Q, K[0], stacks_in, shifted=False)

                def store(n):
                    sp.wait_ge(step, PER * (n + 1))
                    for p in range(RC):
                        sp.dma_start(shifts[bass.ds(n, 1), p, :, :], parts[:, p, :]).then_inc(shift_out, 16)

                with sp.Fori(0, BH - 1) as n:
                    store(n)
                    load_stacks(sp, a, keep, n + 1, Q, K[0], stacks_in, shifted=False)
                store(BH - 1)
                sp.wait_ge(shift_out, 16 * RC * BH + 16)

            @block.tensor
            def _(pe):
                pe.wait_ge(loaded, 64)
                with pe.Fori(0, BH) as n:
                    pe.wait_ge(stacks_in, (LOADS - 16) * (n + 1))
                    pe.wait_ge(k_turned, n + 1)
                    for qt in range(KT):
                        pe.wait_ge(topped, KT * n + qt + 1)
                        for bank in range(BPB):
                            stack = K[0 if bank <= qt // TT else 1]
                            mm = pe.matmul(SC[:, bank, :], Q[:, qt * P:(qt + 1) * P], stack[:, bank * TB:(bank + 1) * TB],
                                           start=True, stop=True)
                        mm.then_inc(scored, 1)
                    pe.wait_ge(topped, KT * (n + 1) + 1)
                    pe.transpose(T[0:KT, 0:P], top[:], ident[:]).then_inc(turned, 1)

            @block.vector
            def _(dve):
                v = nc.vector
                steps = Steps(dve, step, PER)
                dve.sem_inc(topped, 1)
                dve.sem_inc(shift_out, 16)
                dve.wait_ge(loaded, 64)
                with dve.Fori(0, BH) as n:
                    steps.begin(n)
                    dve.wait_ge(stacks_in, (LOADS - 16) * (n + 1))
                    v.tensor_scalar(K[1][:], K[0][:], side[:], None, ALU.mult).then_inc(k_turned, 1)
                    for qt in range(KT):
                        dve.wait_ge(scored, KT * n + qt + 1)
                        at = qt % TT * P
                        sc = SC[:, qt // TT, at:TB]
                        steps(v.scalar_tensor_tensor(out=sc, in0=fold[:, 0:TB - at], scalar=slopes[:, bass.ds(n % H, 1)],
                                                     in1=sc, op0=ALU.mult, op1=ALU.add))
                        v.tensor_reduce(top[:, qt:qt + 1], SC[:], AX.XY, ALU.max).then_inc(topped, 1)
                    dve.wait_ge(turned, n + 1)
                    dve.wait_ge(shift_out, 16 * RC * n + 16)
                    steps(v.tensor_scalar(neg[:], T[0:KT, 0:P], -1.0, None, ALU.mult))
                    steps(v.tensor_copy(parts[:, 0, :], neg[:]))
                    steps(v.tensor_tensor(neg[:], neg[:], parts[:, 0, :], ALU.subtract))
                    steps(v.tensor_copy(parts[:, 1, :], neg[:]))
                    steps(v.tensor_tensor(parts[:, 2, :], neg[:], parts[:, 1, :], ALU.subtract))
                    steps.end()


def output_stage(nc, a, keep, out_dram):
    gate_all = keep["gate_all"]
    with ExitStack() as ctx:
        r = Room(nc, ctx, "out", keep)
        w_o = r.sb("w_o", [P, DC, D])
        b_o = r.sb("b_o", [P, D])
        o = r.sb("o", [P, BPB, DC, TB])
        recip = r.sb("recip", [P, BPB, DC, TB])
        x = r.sb("x", [P, BPB, TT, D])
        y = r.sb("y", [P, BPB, TT, D])
        Z = r.ps("Z", [P, 2, 2, TB])
        loaded = r.sem("loaded")
        block_in = [r.sem(f"block_in{n}") for n in range(BPB)]
        scaled = r.sem("scaled")
        projected = r.sem("projected")
        done = r.sem("done")
        stored = [r.sem(f"stored{n}") for n in range(BPB)]
        step = r.sem("step")
        IN = 16 * (2 * DC + 1)
        sums = keep["sums"].rearrange("(n g r) q -> n g r q", g=BPB, r=VW)
        recips = keep["recips"].rearrange("(n g) q -> n g q", g=BPB)
        tokens = a["x"].rearrange("b s d -> (b s) d")
        results = out_dram.rearrange("b s d -> (b s) d")
        with nc.Block() as block:
            @block.sync
            def _(sp):
                sp.dma_start(w_o[:], a["wT_out"].rearrange("(c p) n -> p c n", p=P)).then_inc(loaded, 16)
                sp.dma_start(b_o[:], a["b_out"].rearrange("(o n) -> o n", o=1).broadcast_to([P, D])).then_inc(loaded, 16)
                with sp.Fori(0, B) as b:
                    for g in range(BPB):
                        j, u = b * BPB + g, g
                        sp.wait_ge(done, j + 1)
                        sem = block_in[u]
                        for c in range(DC):
                            heads = bass.ds(b * H + 8 * c, 8)
                            sp.dma_start(o[:, u, c, :], sums[heads, g, 0:HD, :]).then_inc(sem, 16)
                            sp.dma_start(recip[:, u, c, :], recips[heads, g, :].unsqueeze(1).broadcast_to([8, HD, TB])).then_inc(sem, 16)
                        sp.dma_start(x[:, u], tokens[bass.ds(j * TB, TB), :].rearrange("(t p) d -> p t d", p=P)).then_inc(sem, 16)

            @block.scalar
            def _(act):
                with act.Fori(0, B) as b:
                    for g in range(BPB):
                        j, u = b * BPB + g, g
                        act.wait_ge(done, j + 1 + BPB)
                        act.dma_start(results[bass.ds(j * TB, TB), :].rearrange("(t p) d -> p t d", p=P), y[:, u]).then_inc(stored[u], 16)
                for u in range(BPB):
                    act.wait_ge(stored[u], 16 * (B + 1))

            @block.tensor
            def _(pe):
                pe.wait_ge(loaded, 32)
                with pe.Fori(0, B) as b:
                    for g in range(BPB):
                        j, u = b * BPB + g, g
                        pe.wait_ge(scaled, j + 1)
                        pe.wait_ge(done, j + 3)
                        for t in range(TT):
                            for c in range(DC):
                                mm = pe.matmul(Z[:, u % 2, t // 2, t % 2 * D:(t % 2 + 1) * D], o[:, u, c, t * P:(t + 1) * P],
                                               w_o[:, c, :], start=(c == 0), stop=(c == DC - 1))
                        mm.then_inc(projected, 1)

            @block.vector
            def _(dve):
                v = nc.vector
                steps = Steps(dve, step, 2 * BPB)

                def scale(b, g):
                    u = g
                    dve.wait_ge(block_in[u], IN * (b + 1))
                    v.tensor_tensor(o[:, u], o[:, u], recip[:, u], ALU.mult).then_inc(scaled, 1)

                def finish(b, g):
                    j, u = b * BPB + g, g
                    dve.wait_ge(projected, j + 1)
                    dve.wait_ge(stored[u], 16 * b + 16)
                    yy = y[:, u]
                    steps(v.tensor_tensor(yy, Z[:, u % 2].rearrange("p a (b d) -> p (a b) d", d=D),
                                          b_o[:].unsqueeze(1).broadcast_to([P, TT, D]), ALU.add))
                    steps(v.tensor_tensor(yy, yy, gate_all[:, bass.ds(j * TT, TT), :], ALU.mult))
                    v.tensor_tensor(yy, yy, x[:, u], ALU.add).then_inc(done, 1)

                dve.sem_inc(done, BPB)
                for u in range(BPB):
                    dve.sem_inc(stored[u], 16)
                dve.wait_ge(loaded, 32)
                scale(0, 0)
                with dve.Fori(0, B - 1) as b:
                    steps.begin(b)
                    for g in range(BPB):
                        scale(b + (g + 1) // BPB, (g + 1) % BPB)
                        finish(b, g)
                    steps.end()
                steps.begin(B - 1)
                for g in range(BPB):
                    if g < BPB - 1:
                        scale(B - 1, g + 1)
                    finish(B - 1, g)
                steps.end()


def build(nc, a, out):
    with ExitStack() as ctx:
        scratch = lambda name, shape, dt: nc.dram_tensor(name, shape, dt).ap()
        keep = {
            "whole": ctx,
            "v_all": ctx.enter_context(nc.sbuf_tensor("v_all", [P, NBLK * TT, D], F32)),
            "gate_all": ctx.enter_context(nc.sbuf_tensor("gate_all", [P, NBLK * TT, D], F32)),
            "redo": ctx.enter_context(nc.sbuf_tensor("redo", [1, 1], I32)),
            "q_parts": scratch("q_parts", (BH * 3 * HD, S), BF16),
            "k_parts": scratch("k_parts", (BH * 3 * HD, S), BF16),
            "shifts": scratch("shifts", (BH * RC, S), BF16),
            "sums": scratch("sums", (BH * P, TB), F32),
            "recips": scratch("recips", (BH * BPB, TB), F32),
        }
        tokens_stage(nc, a, keep)
        attention_stage(nc, a, keep, "own")
        sums_stage(nc, keep, "own")
        redo = nc.values_load(keep["redo"][0:1, 0:1], min_val=0, max_val=1)
        with nc.If(redo != 0):
            maximum_stage(nc, a, keep)
            attention_stage(nc, a, keep, "top")
            sums_stage(nc, keep, "top")
        output_stage(nc, a, keep, out)


NAMES = {
    "x": "L0_attn_x", "b_qkv": "L0_attn_b_qkv", "b_out": "L0_attn_b_out",
    "correction_bias": "L0_ffn_correction_bias", "w_gate": "L0_ffn_w_gate", "w_up": "L0_ffn_w_up",
    "w_down": "L0_ffn_w_down", "sw_gate": "L0_ffn_sw_gate", "sw_up": "L0_ffn_sw_up", "sw_down": "L0_ffn_sw_down",
}
TURNED = {"wT_qkv": "L0_attn_W_qkv", "wT_out": "L0_attn_W_out", "wT_router": "L0_ffn_router_weight"}


def kernel(**inputs):
    import concourse.bacc as bacc
    from concourse.bass_utils import run_bass_kernel_spmd

    nc = bacc.Bacc("TRN2", target_bir_lowering=False, num_devices=1)
    arrays = {k: np.ascontiguousarray(inputs[n]) for k, n in NAMES.items()}
    arrays |= {k: np.ascontiguousarray(np.transpose(inputs[n])) for k, n in TURNED.items()}
    arrays |= {k: np.ascontiguousarray(c) for k, c in constants().items()}
    a = {k: nc.dram_tensor(f"in_{k}", v.shape, mybir.dt.from_np(v.dtype), kind="ExternalInput").ap()
         for k, v in arrays.items()}
    out = nc.dram_tensor("out", (B, S, D), F32, kind="ExternalOutput").ap()
    build(nc, a, out)
    result = run_bass_kernel_spmd(nc, [{f"in_{k}": v for k, v in arrays.items()}], core_ids=[0])
    return result.results[0]["out"]
```

```python
from contextlib import ExitStack

import numpy as np

import concourse.bass as bass
from concourse import mybir

ALU = mybir.AluOpType
ACT = mybir.ActivationFunctionType
AX = mybir.AxisListType
RMAX = bass.bass_isa.ReduceOp.max
F32 = mybir.dt.float32
BF16 = mybir.dt.bfloat16
F16 = mybir.dt.float16
U16 = mybir.dt.uint16
I32 = mybir.dt.int32

P = 128
B, S, D = 4, 2048, 256
H, HD = 16, 16
E, I = 8, 128
NE = E + 1
BH = B * H
DC = D // P
TB = 512
NBLK = B * S // TB
BPB = S // TB
TT = TB // P
KT = S // P
PAIRS = 6
RB = 12
RC = 3
RS = 13
R0 = RS + RC
ROWS = R0 + PAIRS * HD
DEPTH = 4
TILES = 2 * KT
RING = 3
XS = 2.0 ** 11
VW = 32
EXPERTS = (E, *range(E))
LIFT = 32.0
LEAST_RECIP, MOST_RECIP = 2.0 ** -100, 2.0 ** 48
QUARTER_AT, EXTREMES_AT, DIVIDE_AT = (3, 4, 5, 6), 7, 14
TURN_K_AT = 13


def bf16_parts(a):
    parts, rest = [], np.asarray(a, np.float32)
    for _ in range(3):
        part = (rest.view(np.uint32) & np.uint32(0xFFFF0000)).view(np.float32)
        parts.append(part)
        rest = (rest - part).astype(np.float32)
    return parts


def ring_slots():
    cold = [t for t in range(2 * TILES) if t % 2 != t % TILES // KT]
    for first in cold[4:]:
        for second in cold:
            if second < first + KT:
                continue
            order, slots = list(range(RING)), []
            for t in range(2 * TILES):
                slot = order.pop(1 if t in (first, second) else 0)
                order.append(slot)
                slots.append(slot)
            if order == list(range(RING)):
                back = [next(d for d in range(1, 9) if slots[t - d] == slots[t]) for t in range(2 * TILES)]
                return slots, back


def constants():
    slope = np.power(np.float32(2), np.float32(8) * -np.arange(H, dtype=np.float32) / np.float32(H)).astype(np.float32)
    pos = np.arange(S, dtype=np.float32)
    hi, lo = np.floor(pos / P) * P, pos % P
    ones = np.ones(S, np.float32)
    q_rows = np.zeros((H, RS, S), np.float32)
    k_rows = np.zeros((H, R0, S), np.float32)
    for h in range(H):
        for n, part in enumerate(bf16_parts(slope[h:h + 1])):
            q_rows[h, 4 * n:4 * n + 4] = [part * ones, part * ones, hi, lo]
            k_rows[h, 4 * n:4 * n + 4] = [hi, lo, -part * ones, -part * ones]
        k_rows[h, RS:R0] = 1.0
    j, k = np.arange(TB, dtype=np.float32), np.arange(P, dtype=np.float32)
    side = np.ones((ROWS, 1), np.float32)
    side[:RB] = -1.0
    head_of = np.zeros((P, DC, H), np.float32)
    for c in range(DC):
        head_of[np.arange(P), c, 8 * c + np.arange(P) // HD] = 1.0
    low = (np.arange(E)[None, :] < np.arange(E)[:, None]).astype(np.float32)
    as_bf16 = lambda a: (np.ascontiguousarray(a).view(np.uint32) >> 16).astype(np.uint16)
    return {
        "q_rows": as_bf16(q_rows).reshape(H * RS, S),
        "k_rows": as_bf16(k_rows).reshape(H * R0, S),
        "fold": (-2 * np.maximum(j[None] - k[:, None], 0)).astype(np.float32),
        "slopes": np.tile(slope[None], (P, 1)),
        "side": side,
        "head_of": head_of,
        "chosen": (np.arange(P) % VW == HD).astype(np.float32).reshape(P, 1),
        "lower": np.tile(low.reshape(1, E, E), (P, 1, 1)),
        "ident": np.eye(P, dtype=np.float32),
    }


class Room:

    def __init__(self, nc, ctx, tag, keep):
        self.nc, self.ctx, self.tag, self.whole = nc, ctx, tag, keep["whole"]

    def sb(self, name, shape, dt=F32):
        return self.ctx.enter_context(self.nc.sbuf_tensor(f"{name}_{self.tag}", shape, dt))

    def ps(self, name, shape, dt=F32):
        return self.ctx.enter_context(self.nc.psum_tensor(f"{name}_{self.tag}", shape, dt))

    def sem(self, name):
        return self.whole.enter_context(self.nc.semaphore(f"{name}_{self.tag}"))


class Steps:

    def __init__(self, engine, sem, per):
        self.engine, self.sem, self.per = engine, sem, per

    def begin(self, turn):
        self.turn, self.k = turn, 0

    def __call__(self, ins):
        self.k += 1
        ins.then_inc(self.sem, 1)
        self.engine.wait_ge(self.sem, self.turn * self.per + self.k)

    def end(self):
        assert self.k == self.per, (self.k, self.per)


def tokens_stage(nc, a, keep):
    x_all, gate_all = keep["x_all"], keep["gate_all"]
    with ExitStack() as ctx:
        r = Room(nc, ctx, "tok", keep)
        ident = r.sb("ident", [P, P])
        head_of = r.sb("head_of", [P, DC, H])
        lower = r.sb("lower", [P, E, E])
        w_qkv = r.sb("w_qkv", [P, 2, DC, 3 * D], F16)
        w_r = r.sb("w_r", [P, 2, DC, E], F16)
        w_gu = r.sb("w_gu", [P, 2, DC, 2, NE, I], F16)
        flat = gate_all[:].rearrange("p t d -> p (t d)")
        at_gu = NBLK * TT * D // 2
        at_qkv = at_gu + 2 * DC * NE * I
        at_r = at_qkv + DC * 3 * D
        raw_gu = flat[:, at_gu:at_qkv].rearrange("p (c w e i) -> p c w e i", w=2, c=DC, e=NE)
        raw_qkv = flat[:, at_qkv:at_r].rearrange("p (c n) -> p c n", c=DC)
        raw_r = flat[:, at_r:at_r + DC * E].rearrange("p (c n) -> p c n", c=DC)
        flat_gu = lambda c: flat[:, at_gu + 2 * c * NE * I:at_gu + 2 * (c + 1) * NE * I]
        size_gu = lambda c: flat[:, 2048 + 2 * c * NE * I:2048 + 2 * (c + 1) * NE * I]
        size_qkv, size_r = flat[:, 0:DC * 3 * D], flat[:, DC * 3 * D:DC * (3 * D + E)]
        peak = r.sb("peak", [P, 4])
        power = r.sb("power", [P, 4])
        scale = r.sb("scale", [P, 3])
        undo = r.sb("undo", [P, 3])
        undo_q = r.sb("undo_q", [P, 1])
        w_d = r.sb("w_d", [P, NE, D])
        b_qk = r.sb("b_qk", [P, 2 * DC])
        b_v = r.sb("b_v", [P, D])
        b_c = r.sb("b_c", [P, E])
        b_o = r.sb("b_o", [P, D])
        gated_b = r.sb("gated_b", [P, 1, D])
        x = r.sb("x", [P, TT, D])
        v_block = r.sb("v_block", [P, H, TT, HD])
        xT = r.sb("xT", [P, 2, 2, DC, TB], F16)
        stats = r.sb("stats", [P, TT, 6])
        mv = r.sb("mv", [P, TT, 2])
        var = r.sb("var", [P, TT])
        std = r.sb("std", [P, TT])
        rstd = r.sb("rstd", [P, TT])
        qk = r.sb("qk", [P, 2 * DC, TB])
        rest = r.sb("rest", [P, TB])
        parts = r.sb("parts", [P, 2, 3, TB], BF16)
        shift = r.sb("shift", [H, 3, TB], BF16)
        hid = r.sb("hid", [P, 2, TB])
        score = r.sb("score", [P, TT, E])
        choice = r.sb("choice", [P, TT, E])
        pair = r.sb("pair", [P, TT * 2, 6])
        group = r.sb("group", [P, TT * 2])
        gmask = r.sb("gmask", [P, TT, 2])
        beat = r.sb("beat", [P, TT, E, E])
        tie = r.sb("tie", [P, TT, E, E])
        rank = r.sb("rank", [P, TT, E])
        comb = r.sb("comb", [P, TT, E])
        wsum = r.sb("wsum", [P, TT])
        wrec = r.sb("wrec", [P, TT])
        idle = r.sb("idle", [P, 1])
        act_idle = r.sb("act_idle", [P, 1])

        T = r.ps("T", [P, DC, TB])
        GU = r.ps("GU", [P, 4, TB])
        Y = r.ps("Y", [P, 2, TB])

        PRODUCTS = [(c, w, x) for c in range(DC) for w, x in ((0, 0), (0, 1), (1, 0))]
        ORDER = (2, 3, 0, 1)
        SPLIT_AT = {1: 1, 2: 2, 4: 3}
        OWN_AT, STATS_AT, NORM_AT, SHIFT_AT, TURN_AT = 4, 3, 5, 6, 7
        loaded = r.sem("loaded")
        x_in = r.sem("x_in")
        var_ready = r.sem("var_ready")
        std_ready = r.sem("std_ready")
        xn_ready = r.sem("xn_ready")
        turned = r.sem("turned")
        xT_high = r.sem("xT_high")
        xT_low = r.sem("xT_low")
        raw_in = r.sem("raw_in")
        raw_gu_in = [r.sem(f"raw_gu_in{c}") for c in range(DC)]
        sized = r.sem("sized")
        peaked = r.sem("peaked")
        topped = r.sem("topped")
        scaled = r.sem("scaled")
        w_high = r.sem("w_high")
        w_low = r.sem("w_low")
        qk_mm = r.sem("qk_mm")
        v_mm = r.sem("v_mm")
        logit_mm = r.sem("logit_mm")
        own_mm = r.sem("own_mm")
        qk_out = r.sem("qk_out")
        v_out = r.sem("v_out")
        v_stored = r.sem("v_stored")
        part1 = r.sem("part1")
        rest_ready = r.sem("rest_ready")
        part2 = r.sem("part2")
        part3 = r.sem("part3")
        parts_out = [r.sem(f"parts_out{n}") for n in range(2)]
        sig = r.sem("sig")
        own_ready = r.sem("own_ready")
        own_read = r.sem("own_read")
        shift_ready = r.sem("shift_ready")
        shift_out = r.sem("shift_out")
        gu_mm = r.sem("gu_mm")
        silu = r.sem("silu")
        hid_ready = r.sem("hid_ready")
        down_mm = r.sem("down_mm")
        added = r.sem("added")
        gate_out = r.sem("gate_out")
        dve_step = r.sem("dve_step")
        ln_step = r.sem("ln_step")
        pool_step = r.sem("pool_step")

        wT = a["wT_qkv"].rearrange("(c p) n -> p c n", p=P)
        first_loads = [(ident[:], a["ident"]), (raw_qkv, wT), (raw_r, a["wT_router"].rearrange("(c p) n -> p c n", p=P))]
        gu_loads = []
        for c in range(DC):
            rows = slice(c * P, (c + 1) * P)
            for n, (w, sw) in enumerate((("w_gate", "sw_gate"), ("w_up", "sw_up"))):
                gu_loads += [(raw_gu[:, c, n, 0:E, :], a[w][:, rows, :].rearrange("e p i -> p e i")),
                             (raw_gu[:, c, n, E, :], a[sw][rows, :])]
        loads = [
            (b_qk[:], a["b_qkv"].rearrange("(c p) -> p c", p=P)[:, 0:2 * DC]),
            (b_v[:], a["b_qkv"].rearrange("(o n) -> o n", o=1)[:, 2 * D:3 * D].broadcast_to([P, D])),
            (b_o[:], a["b_out"].rearrange("(o n) -> o n", o=1).broadcast_to([P, D])),
            (b_c[:], a["correction_bias"].rearrange("(o n) -> o n", o=1).broadcast_to([P, E])),
            (head_of[:], a["head_of"]), (lower[:], a["lower"]),
            (w_d[:, 0:E, :], a["w_down"].rearrange("e i h -> i e h")),
            (w_d[:, E, :], a["sw_down"]),
        ]
        ALL_LOADED = 16 * len(loads)

        x_rows = a["x"].rearrange("b s d -> (b s) d")
        q_parts = keep["q_parts"].rearrange("(n p d) s -> n p d s", p=3, d=HD)
        k_parts = keep["k_parts"].rearrange("(n p d) s -> n p d s", p=3, d=HD)
        v_rows = keep["values"].rearrange("(n p) k -> p n k", p=P)
        shifts = keep["shifts"].rearrange("(n p) s -> n p s", p=RC)

        with nc.Block() as block:
            @block.sync
            def _(sp):
                def load_x(j):
                    sp.dma_start(x_all[:, bass.ds(j * TT, TT), :], x_rows[bass.ds(j * TB, TB), :].rearrange("(t p) d -> p t d", p=P)).then_inc(x_in, 16)

                def store_parts(b, g):
                    j = b * BPB + g
                    for k, m in enumerate(ORDER):
                        dst = (q_parts if m < DC else k_parts)[bass.ds(b * H + 8 * (m % DC), 8), :, :, g * TB:(g + 1) * TB]
                        sp.wait_ge(part1, 4 * j + k + 1)
                        sp.wait_ge(part2, 4 * j + k + 1)
                        sp.wait_ge(part3, 4 * j + k + 1)
                        for n in range(3):
                            sp.dma_start(dst[:, n], parts[:, k % 2, n, :]).then_inc(parts_out[k % 2], 16)
                        if k == 0:
                            sp.wait_ge(v_out, j + 2)
                            sp.dma_start(v_rows[:, bass.ds(b * H, H), g * TT * HD:(g + 1) * TT * HD],
                                         v_block[:].rearrange("p h t d -> p h (t d)")).then_inc(v_stored, 16)
                    sp.wait_ge(shift_ready, j + 1)
                    for n in range(3):
                        sp.dma_start(shifts[bass.ds(b * H, H), n, g * TB:(g + 1) * TB], shift[:, n, :]).then_inc(shift_out, 16)

                load_x(0)
                with nc.allow_non_contiguous_dma(reason="512 biases, once"):
                    for group, sem in ((first_loads, raw_in), (gu_loads[:4], raw_gu_in[0]), (gu_loads[4:], raw_gu_in[1]), (loads, loaded)):
                        for dst, src in group:
                            sp.dma_start(dst, src).then_inc(sem, 16)
                with sp.Fori(0, B - 1) as b:
                    for g in range(BPB):
                        sp.wait_ge(turned, b * BPB + g + 1)
                        load_x(b * BPB + g + 1)
                        store_parts(b, g)
                for g in range(BPB):
                    if g < BPB - 1:
                        sp.wait_ge(turned, (B - 1) * BPB + g + 1)
                        load_x((B - 1) * BPB + g + 1)
                    store_parts(B - 1, g)
                for n in range(2):
                    sp.wait_ge(parts_out[n], 16 + 96 * NBLK)
                sp.wait_ge(shift_out, 16 + 48 * NBLK)
                sp.wait_ge(v_stored, 16 + 16 * NBLK)

            @block.tensor
            def _(pe):
                def gate_up(j, par, e):
                    if e < 2:
                        pe.wait_ge(qk_out, 4 * j + 4 - 2 * e)
                    else:
                        pe.wait_ge(hid_ready, NE * j + e - 1)
                    for n in range(2):
                        for k, (c, w, x) in enumerate(PRODUCTS):
                            mm = pe.matmul(GU[:, 2 * (e % 2) + n, :], w_gu[:, w, c, n, EXPERTS[e], :], xT[:, par, x, c, :],
                                           start=(k == 0), stop=(k == len(PRODUCTS) - 1))
                    mm.then_inc(gu_mm, 1)

                def down(j, e):
                    pe.wait_ge(hid_ready, NE * j + e + 1)
                    if e == 0:
                        pe.wait_ge(sig, j + 1)
                    else:
                        pe.wait_ge(added, NE * j + e)
                    for t in range(TT):
                        mm = pe.matmul(Y[:, t // 2, (t % 2) * D:(t % 2 + 1) * D], hid[:, e % 2, t * P:(t + 1) * P],
                                       w_d[:, EXPERTS[e], :], start=True, stop=True)
                    mm.then_inc(down_mm, 1)

                def turn(j):
                    pe.wait_ge(xn_ready, j + 1)
                    pe.wait_ge(v_out, j + 1)
                    pe.wait_ge(own_read, j + 1)
                    for c in range(DC):
                        for t in range(TT):
                            mm = pe.transpose(T[:, c, t * P:(t + 1) * P], x[:, t, c * P:(c + 1) * P], ident[:])
                    mm.then_inc(turned, 1)

                def chunks(par, ms):
                    for m in ms:
                        for k, (c, w, x) in enumerate(PRODUCTS):
                            mm = pe.matmul(GU[:, m, :], w_qkv[:, w, c, m * P:(m + 1) * P], xT[:, par, x, c, :],
                                           start=(k == 0), stop=(k == len(PRODUCTS) - 1))
                        mm.then_inc(qk_mm, 1)

                def k_chunks(j, par):
                    pe.wait_ge(xT_high, 2 * j + 2)
                    pe.wait_ge(xT_low, j + 1)
                    chunks(par, ORDER[:2])

                def body(j, par, last):
                    chunks(par, ORDER[2:])
                    for t in range(TT):
                        for k, (c, w, x) in enumerate(PRODUCTS):
                            mm = pe.matmul(T[:, t // 2, (t % 2) * D:(t % 2 + 1) * D], xT[:, par, x, c, t * P:(t + 1) * P],
                                           w_qkv[:, w, c, 2 * D:3 * D], start=(k == 0), stop=(k == len(PRODUCTS) - 1))
                    mm.then_inc(v_mm, 1)
                    pe.wait_ge(gate_out, j + 1)
                    for t in range(TT):
                        for k, (c, w, x) in enumerate(PRODUCTS):
                            mm = pe.matmul(Y[:, 0, t * E:(t + 1) * E], xT[:, par, x, c, t * P:(t + 1) * P],
                                           w_r[:, w, c, :], start=(k == 0), stop=(k == len(PRODUCTS) - 1))
                    mm.then_inc(logit_mm, 1)
                    pe.wait_ge(w_high, 2 + DC)
                    pe.wait_ge(w_low, 2 + DC)
                    pe.wait_ge(loaded, ALL_LOADED)
                    gate_up(j, par, 0)
                    for e in range(1, NE):
                        gate_up(j, par, e)
                        down(j, e - 1)
                        if e == TURN_AT and not last:
                            turn(j + 1)
                        if e == OWN_AT:
                            pe.wait_ge(own_ready, j + 1)
                            pe.wait_ge(v_out, j + 2)
                            for c in range(DC):
                                mm = pe.matmul(T[0:H, 0, :], head_of[:, c, :], qk[:, DC + c, :], start=(c == 0), stop=(c == DC - 1))
                            mm.then_inc(own_mm, 1)
                    if not last:
                        k_chunks(j + 1, 1 - par)
                    down(j, NE - 1)

                pe.wait_ge(raw_in, 16 * len(first_loads))
                turn(0)
                pe.wait_ge(w_high, 2)
                pe.wait_ge(w_low, 2)
                k_chunks(0, 0)
                with pe.Fori(0, NBLK // 2 - 1) as i:
                    body(2 * i, 0, False)
                    body(2 * i + 1, 1, False)
                body(NBLK - 2, 0, False)
                body(NBLK - 1, 1, True)

            @block.gpsimd
            def _(pool):
                for n, (lo, hi) in enumerate(((0, 2), (2, 3))):
                    pool.wait_ge(peaked, n + 1)
                    nc.gpsimd.partition_all_reduce(power[:, lo:hi], peak[:, lo:hi], P, RMAX).then_inc(topped, 1)
                def split(j):
                    for k, m in enumerate(ORDER):
                        pool.wait_ge(part1, 4 * j + k + 1)
                        pool.wait_ge(qk_out, 4 * j + k + 1)
                        nc.gpsimd.tensor_tensor(rest[:], qk[:, m, :], parts[:, k % 2, 0, :],
                                                ALU.subtract).then_inc(rest_ready, 1)
                        pool.wait_ge(part2, 4 * j + k + 1)
                        pool.wait_ge(rest_ready, 4 * j + k + 1)
                        nc.gpsimd.tensor_tensor(parts[:, k % 2, 2, :], rest[:], parts[:, k % 2, 1, :],
                                                ALU.subtract).then_inc(part3, 1)
                        pool.wait_ge(part3, 4 * j + k + 1)

                def add_bias(j):
                    steps.begin(j)
                    pool.wait_ge(gate_out, j + 1 + 1)
                    for t in range(TT):
                        tiles = bass.ds(j * TT + t, 1)
                        steps(nc.gpsimd.tensor_tensor(gated_b[:], gate_all[:, tiles, :],
                                                      b_o[:].unsqueeze(1), ALU.mult))
                        steps(nc.gpsimd.tensor_tensor(x_all[:, tiles, :], x_all[:, tiles, :], gated_b[:], ALU.add))
                    steps.end()

                steps = Steps(pool, pool_step, 2 * TT)
                split(0)
                pool.wait_ge(loaded, ALL_LOADED)
                with pool.Fori(1, NBLK) as j:
                    split(j)
                    add_bias(j - 1)

            @block.scalar
            def _(act):
                def high(n, dst, src):
                    nc.scalar.activation(dst, src, ACT.Copy, scale=scale[:, n:n + 1]).then_inc(w_high, 1)

                def size(dst, src):
                    nc.scalar.activation(dst, src, ACT.Abs).then_inc(sized, 1)

                def root():
                    return nc.scalar.activation(std[:], var[:], ACT.Sqrt)

                def split(j, k):
                    act.wait_ge(qk_out, 4 * j + k + 1)
                    act.wait_ge(parts_out[k % 2], 96 * j + 48 * (k // 2) + 16)
                    nc.scalar.copy(parts[:, k % 2, 0, :], qk[:, ORDER[k], :]).then_inc(part1, 1)
                    act.wait_ge(rest_ready, 4 * j + k + 1)
                    nc.scalar.copy(parts[:, k % 2, 1, :], rest[:]).then_inc(part2, 1)

                def sum_of(j):
                    return gate_all[:, bass.ds(j * TT, TT), :].rearrange("p t d -> p (t d)")

                def take_xT(j, par):
                    act.wait_ge(turned, j + 1)
                    for c in range(DC):
                        nc.scalar.activation(xT[:, par, 0, c, :], T[:, c, :], ACT.Copy, scale=XS).then_inc(xT_high, 1)

                def body(j, par, last):
                    split(j, 0)
                    for e in range(NE):
                        act.wait_ge(gu_mm, NE * j + e + 1)
                        act.wait_ge(down_mm, NE * j + max(e - 1, 0) + 1)
                        nc.scalar.activation(hid[:, e % 2, :], GU[:, 2 * (e % 2), :], ACT.Silu,
                                             scale=undo[:, 2:3]).then_inc(silu, 1)
                        if e == 0:
                            act.wait_ge(logit_mm, j + 1)
                            nc.scalar.activation(score[:].rearrange("p t e -> p (t e)"), Y[:, 0, 0:TT * E], ACT.Sigmoid,
                                                 scale=undo[:, 1:2]).then_inc(sig, 1)
                        if e == 1:
                            act.wait_ge(down_mm, NE * j + 1 + 1)
                            nc.scalar.copy(sum_of(j), Y[:].rearrange("p a n -> p (a n)")).then_inc(added, 1)
                        if e in SPLIT_AT:
                            split(j, SPLIT_AT[e])
                        if e == TURN_AT and not last:
                            take_xT(j + 1, 1 - par)
                        if e == STATS_AT + 1 and not last:
                            act.wait_ge(var_ready, j + 2)
                            root().then_inc(std_ready, 1)
                    act.wait_ge(added, NE * (j + 1))
                    nc.scalar.copy(act_idle[:], undo[:, 0:1])
                    nc.scalar.activation(sum_of(j), sum_of(j), ACT.Silu).then_inc(gate_out, 1)

                act.sem_inc(parts_out[0], 16)
                act.sem_inc(parts_out[1], 16)
                act.sem_inc(down_mm, 1)
                act.wait_ge(var_ready, 1)
                root().then_inc(std_ready, 1)
                act.wait_ge(raw_in, 16 * len(first_loads))
                size(size_qkv, raw_qkv.rearrange("p c n -> p (c n)"))
                size(size_r, raw_r.rearrange("p c n -> p (c n)"))
                for c in range(DC):
                    act.wait_ge(raw_gu_in[c], 16 * 4)
                    size(size_gu(c), flat_gu(c))
                act.wait_ge(scaled, 1)
                high(0, w_qkv[:, 0], raw_qkv)
                high(1, w_r[:, 0], raw_r)
                take_xT(0, 0)
                act.wait_ge(scaled, 2)
                for c in range(DC):
                    high(2, w_gu[:, 0, c].rearrange("p w e i -> p (w e i)"), flat_gu(c))
                with act.Fori(0, NBLK // 2 - 1) as i:
                    body(2 * i, 0, False)
                    body(2 * i + 1, 1, False)
                body(NBLK - 2, 0, False)
                body(NBLK - 1, 1, True)

            @block.vector
            def _(dve):
                v = nc.vector
                step = Steps(dve, dve_step, 17)
                ln = Steps(dve, ln_step, 3)

                once = Steps(dve, r.sem("dve_once"), 12)
                once.begin(0)

                def peaks(n, sizes, count):
                    dve.wait_ge(sized, count)
                    return v.tensor_reduce(peak[:, n:n + 1], sizes, AX.X, ALU.max)

                def scales(lo, hi, n):
                    dve.wait_ge(topped, n + 1)
                    top, mask = power[:, lo:hi], 0x7F800000
                    once(v.tensor_scalar(top, top, 2.0 ** -96, None, ALU.max))
                    once(v.tensor_scalar(top.bitcast(I32), top.bitcast(I32), mask, None, ALU.bitwise_and))
                    v.tensor_scalar(undo[:, lo:hi], top, 2.0 ** -14 / XS, None, ALU.mult)
                    once(v.reciprocal(scale[:, lo:hi], top))
                    once(v.tensor_scalar(scale[:, lo:hi], scale[:, lo:hi], 2.0 ** 14, None, ALU.mult))
                    v.tensor_scalar(undo_q[:], undo[:, 0:1], HD ** -0.5, None, ALU.mult).then_inc(scaled, 1)

                def low_part(n, w, raw):
                    dve.wait_ge(w_high, n + 1)
                    v.scalar_tensor_tensor(out=w[:, 1], in0=raw, scalar=scale[:, n:n + 1], in1=w[:, 0],
                                           op0=ALU.mult, op1=ALU.subtract).then_inc(w_low, 1)

                def tile_of(j, t):
                    return x_all[:, bass.ds(j * TT + t, 1), :].rearrange("p o d -> p (o d)")

                def ln_stats(j):
                    ln.begin(j)
                    dve.wait_ge(x_in, 16 * (j + 1))
                    for t in range(TT):
                        last = v.bn_stats(stats[:, t, :], tile_of(j, t))
                    ln(last)
                    v.memset(idle[:], 0.0)
                    for t in range(TT):
                        last = v.bn_aggr(mv[:, t, :], stats[:, t, :])
                    ln(last)
                    v.tensor_scalar(var[:], mv[:, :, 1], 1e-5, None, ALU.add).then_inc(var_ready, 1)

                def ln_apply(j):
                    dve.wait_ge(std_ready, j + 1)
                    ln(v.reciprocal(rstd[:], std[:]))
                    for t in range(TT):
                        ins = v.tensor_scalar(x[:, t, :], tile_of(j, t), mv[:, t, 0:1], rstd[:, t:t + 1], ALU.subtract, ALU.mult)
                    ins.then_inc(xn_ready, 1)
                    ln.end()

                def rivals(j):
                    dve.wait_ge(sig, j + 1)
                    step(v.tensor_tensor(choice[:], score[:], b_c[:].unsqueeze(1).broadcast_to([P, TT, E]), ALU.add))
                    c4 = choice[:].rearrange("p t (g k) -> p (t g) k", g=2)
                    v.tensor_tensor(pair[:, :, 0:3], c4[:, :, 0:3], c4[:, :, 1:4], ALU.add)
                    v.tensor_tensor(pair[:, :, 3:5], c4[:, :, 0:2], c4[:, :, 2:4], ALU.add)
                    step(v.tensor_tensor(pair[:, :, 5:6], c4[:, :, 0:1], c4[:, :, 3:4], ALU.add))
                    step(v.tensor_reduce(group[:], pair[:], AX.X, ALU.max))
                    g2 = group[:].rearrange("p (t g) -> p t g", g=2)
                    v.tensor_tensor(gmask[:, :, 0:1], g2[:, :, 0:1], g2[:, :, 1:2], ALU.is_ge)
                    step(v.tensor_tensor(gmask[:, :, 1:2], g2[:, :, 0:1], g2[:, :, 1:2], ALU.is_lt))
                    for g in range(2):
                        ins = v.tensor_tensor(choice[:, :, 4 * g:4 * g + 4], choice[:, :, 4 * g:4 * g + 4],
                                              gmask[:, :, g:g + 1].broadcast_to([P, TT, 4]), ALU.mult)
                    step(ins)
                    me = choice[:].unsqueeze(3).broadcast_to([P, TT, E, E])
                    other = choice[:].unsqueeze(2).broadcast_to([P, TT, E, E])
                    v.tensor_tensor(beat[:], other, me, ALU.is_gt)
                    step(v.tensor_tensor(tie[:], other, me, ALU.is_equal))

                def weights(j):
                    step(v.tensor_tensor(tie[:], tie[:], lower[:].unsqueeze(1).broadcast_to([P, TT, E, E]), ALU.mult))
                    step(v.tensor_tensor(beat[:], beat[:], tie[:], ALU.add))
                    step(v.tensor_reduce(rank[:], beat[:], AX.X, ALU.add))
                    step(v.scalar_tensor_tensor(out=comb[:], in0=rank[:], scalar=1.5, in1=score[:], op0=ALU.is_lt, op1=ALU.mult))
                    step(v.tensor_reduce(wsum[:], comb[:], AX.X, ALU.add))
                    step(v.tensor_scalar(wsum[:], wsum[:], 1e-20, None, ALU.add))
                    step(v.reciprocal(wrec[:], wsum[:]))
                    step(v.tensor_tensor(comb[:], comb[:], wrec[:].unsqueeze(2).broadcast_to([P, TT, E]), ALU.mult))

                def weigh(j, e):
                    dve.wait_ge(down_mm, NE * j + e + 1 + 1)
                    dve.wait_ge(added, NE * j + e)
                    for t in range(TT):
                        x = EXPERTS[e]
                        acc = gate_all[:, bass.ds(j * TT + t, 1), :].rearrange("p o d -> p (o d)")
                        ins = v.scalar_tensor_tensor(out=acc, in0=Y[:, t // 2, (t % 2) * D:(t % 2 + 1) * D],
                                                     scalar=comb[:, t, x:x + 1], in1=acc, op0=ALU.mult, op1=ALU.add)
                    ins.then_inc(added, 1)

                def shifts_of(j):
                    own = qk[0:H, DC, :]
                    dve.wait_ge(own_mm, j + 2)
                    v.tensor_scalar(own, T[0:H, 0, :], -1.0, -LIFT, ALU.mult, ALU.add).then_inc(own_read, 1)
                    dve.wait_ge(own_read, j + 2)
                    dve.wait_ge(shift_out, 48 * j + 16)
                    step(v.tensor_copy(shift[:, 0, :], own))
                    step(v.tensor_tensor(own, own, shift[:, 0, :], ALU.subtract))
                    step(v.tensor_copy(shift[:, 1, :], own))
                    v.tensor_tensor(shift[:, 2, :], own, shift[:, 1, :], ALU.subtract).then_inc(shift_ready, 1)

                def take_xT(j, par):
                    for c in range(DC):
                        dve.wait_ge(xT_high, 2 * j + c + 1)
                        ins = v.scalar_tensor_tensor(out=xT[:, par, 1, c, :], in0=T[:, c, :], scalar=XS, in1=xT[:, par, 0, c, :],
                                                     op0=ALU.mult, op1=ALU.subtract)
                    ins.then_inc(xT_low, 1)

                def body(j, par, last):
                    step.begin(j)
                    for k, m in enumerate(ORDER):
                        dve.wait_ge(qk_mm, 4 * j + k + 1)
                        if k == 0:
                            dve.wait_ge(own_mm, j + 1)
                        v.tensor_scalar(qk[:, m, :], GU[:, m, :], undo_q[:] if m < DC else undo[:, 0:1], b_qk[:, m:m + 1],
                                        ALU.mult, ALU.add).then_inc(qk_out, 1)
                    dve.wait_ge(v_mm, j + 1)
                    dve.wait_ge(v_stored, 16 * j + 16)
                    for t in range(TT):
                        ins = v.scalar_tensor_tensor(out=v_block[:, :, t, :], scalar=undo[:, 0:1], op0=ALU.mult, op1=ALU.add,
                                                     in0=T[:, t // 2, (t % 2) * D:(t % 2 + 1) * D].rearrange("p (h d) -> p h d", d=HD),
                                                     in1=b_v[:].rearrange("p (h d) -> p h d", d=HD))
                    ins.then_inc(v_out, 1)
                    for e in range(NE):
                        dve.wait_ge(silu, NE * j + e + 1)
                        v.scalar_tensor_tensor(out=hid[:, e % 2, :], in0=GU[:, 2 * (e % 2) + 1, :], scalar=undo[:, 2:3],
                                               in1=hid[:, e % 2, :], op0=ALU.mult, op1=ALU.mult).then_inc(hid_ready, 1)
                        if e == 0:
                            rivals(j)
                        if e == 1:
                            weights(j)
                        if e > 1:
                            weigh(j, e - 1)
                        if e == 2:
                            dve.wait_ge(rest_ready, 4 * j + 2)
                            for c in range(DC):
                                ins = v.tensor_tensor(qk[:, DC + c, :], qk[:, c, :], qk[:, DC + c, :], ALU.mult)
                            ins.then_inc(own_ready, 1)
                        if e == STATS_AT and not last:
                            ln_stats(j + 1)
                        if e == NORM_AT and not last:
                            ln_apply(j + 1)
                        if e == SHIFT_AT:
                            shifts_of(j)
                            dve.wait_ge(rest_ready, 4 * j + 4)
                        if e == TURN_AT and not last:
                            take_xT(j + 1, 1 - par)
                    weigh(j, NE - 1)
                    step.end()

                dve.sem_inc(v_out, 1)
                dve.sem_inc(v_stored, 16)
                dve.sem_inc(gate_out, 1)
                dve.sem_inc(own_mm, 1)
                dve.sem_inc(own_read, 1)
                dve.sem_inc(shift_out, 16)
                ln_stats(0)
                ln_apply(0)
                peaks(0, size_qkv, 1)
                peaks(1, size_r, 2).then_inc(peaked, 1)
                scales(0, 2, 0)
                low_part(0, w_qkv, raw_qkv)
                low_part(1, w_r, raw_r)
                take_xT(0, 0)
                for c in range(DC):
                    half = peaks(2 + c, size_gu(c), 3 + c)
                once(half)
                v.tensor_tensor(peak[:, 2:3], peak[:, 2:3], peak[:, 3:4], ALU.max).then_inc(peaked, 1)
                scales(2, 3, 1)
                for c in range(DC):
                    dve.wait_ge(w_high, 2 + c + 1)
                    low = w_gu[:, 1, c].rearrange("p w e i -> p (w e i)")
                    high = w_gu[:, 0, c].rearrange("p w e i -> p (w e i)")
                    v.scalar_tensor_tensor(out=low, in0=flat_gu(c), scalar=scale[:, 2:3], in1=high,
                                           op0=ALU.mult, op1=ALU.subtract).then_inc(w_low, 1)
                dve.wait_ge(loaded, ALL_LOADED)
                once(v.tensor_scalar(b_qk[:, 0:DC], b_qk[:, 0:DC], HD ** -0.5, None, ALU.mult))
                with dve.Fori(0, NBLK // 2 - 1) as i:
                    body(2 * i, 0, False)
                    body(2 * i + 1, 1, False)
                body(NBLK - 2, 0, False)
                body(NBLK - 1, 1, True)
                tiles = slice((NBLK - 1) * TT, NBLK * TT)
                dve.wait_ge(gate_out, NBLK + 1)
                once(v.tensor_tensor(x[:], gate_all[:, tiles, :], b_o[:].unsqueeze(1).broadcast_to([P, TT, D]), ALU.mult))
                once(v.tensor_tensor(x_all[:, tiles, :], x_all[:, tiles, :], x[:], ALU.add))
                once.end()


def load_stacks(engine, a, keep, n, Q, K, sem, shifted=True):
    q, k = keep["q_parts"], keep["k_parts"]
    first, head = n * (3 * HD), n % H
    engine.dma_start(Q[0:RS, :].bitcast(U16), a["q_rows"][bass.ds(head * RS, RS), :]).then_inc(sem, 16)
    engine.dma_start(K[0:R0, :].bitcast(U16), a["k_rows"][bass.ds(head * R0, R0), :]).then_inc(sem, 16)
    if shifted:
        engine.dma_start(Q[RS:R0, :], keep["shifts"][bass.ds(n * RC, RC), :]).then_inc(sem, 16)
    at = R0
    for part in range(3):
        rows = (3 - part) * HD
        engine.dma_start(Q[at:at + rows, :], q[bass.ds(first, rows), :]).then_inc(sem, 16)
        same = k[bass.ds(first + part * HD, HD), :].unsqueeze(0).broadcast_to([3 - part, HD, S])
        engine.dma_start(K[at:at + rows, :], same).then_inc(sem, 16)
        at += rows


LOADS = 16 * 9


def attention_stage(nc, a, keep, tag):
    SLOT, BACK = ring_slots()
    with ExitStack() as ctx:
        r = Room(nc, ctx, tag, keep)
        Q = [r.sb(f"Q{n}", [ROWS, S], BF16) for n in range(2)]
        K = [[r.sb(f"K{n}{s}", [ROWS, S], BF16) for s in range(2)] for n in range(2)]
        V_raw = [r.sb(f"V_raw{n}", [P, KT, HD]) for n in range(2)]
        V = [r.sb(f"V{n}", [P, KT, VW]) for n in range(2)]
        probs = [r.sb(f"probs{n}", [P, S]) for n in range(DEPTH)]
        out = [r.sb(f"out{n}", [P, TB]) for n in range(2)]
        fold = r.sb("fold", [P, TB])
        slopes = r.sb("slopes", [P, H])
        side = r.sb("side", [ROWS, 1])
        recip = r.sb("recip", [P, TB])
        recip_all = r.sb("recip_all", [P, TB])
        least = r.sb("least", [P, TB])
        most = r.sb("most", [P, TB])
        fine = r.sb("fine", [P, 1])
        chosen = r.sb("chosen", [P, 1])
        SC = r.ps("SC", [P, RING, 2, TB])
        O = r.ps("O", [P, 2, TB])

        loaded = r.sem("loaded")
        v_ones = r.sem("v_ones")
        stacks_in = [r.sem(f"stacks_in{n}") for n in range(2)]
        k_turned = r.sem("k_turned")
        v_loaded = [r.sem(f"v_loaded{n}") for n in range(2)]
        v_in = r.sem("v_in")
        scored = r.sem("scored")
        folded = r.sem("folded")
        expd = r.sem("expd")
        pv = r.sem("pv")
        out_ready = r.sem("out_ready")
        recip_ready = r.sem("recip_ready")
        recip_out = r.sem("recip_out")
        recip_in = r.sem("recip_in")
        divided = r.sem("divided")
        extreme = r.sem("extreme")
        step, counted = r.sem("step"), r.sem("counted")
        o_out = [r.sem(f"o_out{n}") for n in range(2)]

        with nc.Block() as block:
            @block.sync
            def _(sp):
                def load_v(n, par):
                    sp.dma_start(V_raw[par][:].rearrange("p t d -> p (t d)"), keep["values"][bass.ds(n * P, P), :]).then_inc(v_loaded[par], 16)

                def store(n, par):
                    sp.wait_ge(recip_ready, 4 * (n + 1))
                    lines = keep["recips"][bass.ds(n * BPB, BPB), :]
                    sp.dma_start(lines, recip[HD:P:VW, :]).then_inc(recip_out, 16)
                    sp.wait_ge(recip_out, 16 * (n + 1))
                    sp.dma_start(recip_all[:], lines.unsqueeze(1).broadcast_to([BPB, VW, TB])).then_inc(recip_in, 16)
                    sp.wait_ge(divided, n + 1)
                    sp.dma_start(keep["heads"][bass.ds(n * P, P), :], out[par][:]).then_inc(o_out[par], 16)

                load_stacks(sp, a, keep, 0, Q[0], K[0][0], stacks_in[0])
                for dst, src in ((side[:], a["side"]), (fold[:], a["fold"]), (slopes[:], a["slopes"]), (chosen[:], a["chosen"])):
                    sp.dma_start(dst, src).then_inc(loaded, 16)
                load_v(0, 0)
                load_stacks(sp, a, keep, 1, Q[1], K[1][0], stacks_in[1])
                load_v(1, 1)
                with sp.Fori(0, BH // 2 - 1) as i:
                    for par in range(2):
                        sp.wait_ge(scored, TILES * (2 * i + par + 1))
                        load_stacks(sp, a, keep, 2 * i + par + 2, Q[par], K[par][0], stacks_in[par])
                        sp.wait_ge(v_in, 2 * i + par + 1)
                        load_v(2 * i + par + 2, par)
                        store(2 * i + par, par)
                for par in range(2):
                    store(BH - 2 + par, par)
                for par in range(2):
                    sp.wait_ge(o_out[par], 16 * (BH // 2 + 1))

            @block.gpsimd
            def _(pool):
                def stage_v(turn, par):
                    pool.wait_ge(v_loaded[par], 16 * (turn + 1))
                    nc.gpsimd.tensor_tensor(V[par][:, :, 0:HD], V_raw[par][:], V[par][:, :, HD:VW], ALU.mult).then_inc(v_in, 1)

                for n in range(2):
                    nc.gpsimd.memset(V[n][:], 1.0)
                nc.gpsimd.drain().then_inc(v_ones, 1)
                pool.wait_ge(v_ones, 1)
                for par in range(2):
                    stage_v(0, par)
                with pool.Fori(1, BH // 2) as i:
                    for par in range(2):
                        pool.wait_ge(pv, KT * (2 * i + par - 1) + DEPTH)
                        stage_v(i, par)

            @block.tensor
            def _(pe):
                def scores(n, turn, par, t):
                    kt, half = t // 2, t % 2
                    if t == 0:
                        pe.wait_ge(stacks_in[par], LOADS * (turn + 1))
                        pe.wait_ge(k_turned, n + 1)
                    pe.wait_ge(expd, TILES * n + t - BACK[par * TILES + t] + 1 + RING)
                    for x in range(2):
                        bank = 2 * half + x
                        stack = K[par][0 if bank > kt // TT else 1]
                        mm = pe.matmul(SC[:, SLOT[par * TILES + t], x, :], stack[:, kt * P:(kt + 1) * P],
                                       Q[par][:, bank * TB:(bank + 1) * TB], start=True, stop=True)
                    mm.then_inc(scored, 1)

                def weighted_sum(n, par, kt):
                    if kt == 0:
                        pe.wait_ge(v_in, n + 1)
                        pe.wait_ge(out_ready, n + 1)
                    pe.wait_ge(expd, TILES * n + 2 * kt + 2 + RING)
                    for g in range(BPB):
                        mm = pe.matmul(O[VW * g:VW * (g + 1), par, :], V[par][:, kt, :],
                                       probs[kt % DEPTH][:, g * TB:(g + 1) * TB], start=(kt == 0), stop=(kt == KT - 1))
                    mm.then_inc(pv, 1)

                def body(i, last):
                    for par in range(2):
                        n = 2 * i + par
                        for kt in range(KT):
                            fold_even = (2 * kt + 4) % TILES < KT
                            for half in range(2):
                                t = 2 * kt + 4 + half
                                if t < TILES:
                                    scores(n, i, par, t)
                                elif par == 0:
                                    scores(n + 1, i, 1, t - TILES)
                                elif not last:
                                    scores(n + 1, i + 1, 0, t - TILES)
                                if half == (0 if fold_even else 1):
                                    weighted_sum(n, par, kt)

                pe.wait_ge(v_ones, 1)
                for t in range(4):
                    scores(0, 0, 0, t)
                with pe.Fori(0, BH // 2 - 1) as i:
                    body(i, False)
                body(BH // 2 - 1, True)
                pe.wait_ge(loaded, 64)
                pe.wait_ge(step, 4)
                pe.matmul(SC[0:1, 0, 0, 0:1], fine[:], chosen[:], start=True, stop=True).then_inc(counted, 1)

            @block.scalar
            def _(act):
                act.sem_inc(expd, RING)
                act.sem_inc(pv, DEPTH)
                act.sem_inc(out_ready, 2)
                with act.Fori(0, BH // 2) as i:
                    for par in range(2):
                        n = 2 * i + par
                        for t in range(TILES):
                            kt, half = t // 2, t % 2
                            if half == kt // TT // 2:
                                act.wait_ge(folded, KT * n + kt + 1)
                            else:
                                act.wait_ge(scored, TILES * n + t + 1)
                            if half == 0:
                                act.wait_ge(pv, KT * n + kt + 1)
                            nc.scalar.activation(probs[kt % DEPTH][:, half * 2 * TB:(half + 1) * 2 * TB],
                                                 SC[:, SLOT[par * TILES + t]].rearrange("p a b -> p (a b)"), ACT.Exp).then_inc(expd, 1)

            @block.vector
            def _(dve):
                v = nc.vector

                def turn_k(n, turn, par):
                    dve.wait_ge(stacks_in[par], LOADS * (turn + 1))
                    v.tensor_scalar(K[par][1][:], K[par][0][:], side[:], None, ALU.mult).then_inc(k_turned, 1)

                def fold_bias(n, par, kt):
                    bank, at = kt // TT, kt % TT * P
                    t = 2 * kt + bank // 2
                    dve.wait_ge(scored, TILES * n + t + 1)
                    sc = SC[:, SLOT[par * TILES + t], bank % 2, at:TB]
                    v.scalar_tensor_tensor(out=sc, in0=fold[:, 0:TB - at], scalar=slopes[:, bass.ds(n % H, 1)],
                                           in1=sc, op0=ALU.mult, op1=ALU.add).then_inc(folded, 1)

                def read_out(n, turn, par):
                    dve.wait_ge(pv, KT * (n + 1) + DEPTH)
                    dve.wait_ge(o_out[par], 16 * turn + 16)
                    v.tensor_copy(out[par][:], O[:, par, :]).then_inc(out_ready, 1)

                def reciprocals(n, par, q):
                    dve.wait_ge(out_ready, n + 1 + 2)
                    at = slice(q * P, (q + 1) * P)
                    v.reciprocal(recip[:, at], out[par][:, at]).then_inc(recip_ready, 1)

                def extremes(n):
                    dve.wait_ge(recip_ready, 4 * (n + 1))
                    dve.wait_ge(extreme, n + 1)
                    v.tensor_tensor(least[:], least[:], recip[:], ALU.min)
                    v.tensor_tensor(most[:], most[:], recip[:], ALU.max).then_inc(extreme, 1)

                def divide(n, par):
                    dve.wait_ge(recip_in, 16 * (n + 1))
                    v.tensor_tensor(out[par][:], out[par][:], recip_all[:], ALU.mult).then_inc(divided, 1)

                def body(i, last, first=False):
                    for par in range(2):
                        n, more = 2 * i + par, par == 0 or not last
                        for kt in range(2, KT):
                            fold_bias(n, par, kt)
                            if not (first and par == 0):
                                if kt in QUARTER_AT:
                                    reciprocals(n - 1, 1 - par, QUARTER_AT.index(kt))
                                if kt == EXTREMES_AT:
                                    extremes(n - 1)
                                if kt == DIVIDE_AT:
                                    divide(n - 1, 1 - par)
                            if kt == TURN_K_AT and more:
                                turn_k(n + 1, i + par, 1 - par)
                        if more:
                            fold_bias(n + 1, 1 - par, 0)
                            fold_bias(n + 1, 1 - par, 1)
                        read_out(n, i, par)

                for par in range(2):
                    dve.sem_inc(o_out[par], 16)
                v.memset(least[:], 1.0)
                v.memset(most[:], 1.0).then_inc(extreme, 1)
                dve.wait_ge(loaded, 64)
                turn_k(0, 0, 0)
                fold_bias(0, 0, 0)
                fold_bias(0, 0, 1)
                body(0, False, True)
                with dve.Fori(1, BH // 2 - 1) as i:
                    body(i, False)
                body(BH // 2 - 1, True)
                steps = Steps(dve, step, 5)
                steps.begin(0)
                for q in range(4):
                    reciprocals(BH - 1, 1, q)
                extremes(BH - 1)
                divide(BH - 1, 1)
                dve.wait_ge(extreme, BH + 1)
                steps(v.tensor_scalar(most[:], most[:], MOST_RECIP, None, ALU.is_le))
                steps(v.tensor_scalar(least[:], least[:], LEAST_RECIP, None, ALU.is_ge))
                steps(v.tensor_tensor(least[:], least[:], most[:], ALU.mult))
                steps(v.tensor_reduce(fine[:], least[:], AX.X, ALU.min))
                dve.wait_ge(counted, 1)
                steps(v.tensor_scalar(keep["redo"][0:1, :], SC[0:1, 0, 0, 0:1], BPB - 0.5, None, ALU.is_lt))
                steps.end()


def maximum_stage(nc, a, keep):
    with ExitStack() as ctx:
        r = Room(nc, ctx, "max", keep)
        Q = r.sb("Q", [ROWS, S], BF16)
        K = [r.sb(f"K{s}", [ROWS, S], BF16) for s in range(2)]
        fold = r.sb("fold", [P, TB])
        slopes = r.sb("slopes", [P, H])
        side = r.sb("side", [ROWS, 1])
        ident = r.sb("ident", [P, P])
        top = r.sb("top", [P, KT])
        neg = r.sb("neg", [KT, P])
        parts = r.sb("parts", [KT, RC, P], BF16)
        SC = r.ps("SC", [P, BPB, TB])
        T = r.ps("T", [P, TB])
        loaded, zeroed, stacks_in, k_turned = r.sem("loaded"), r.sem("zeroed"), r.sem("stacks_in"), r.sem("k_turned")
        scored, topped, turned, shift_out, step = (r.sem("scored"), r.sem("topped"), r.sem("turned"),
                                                   r.sem("shift_out"), r.sem("step"))
        PER = KT + 5
        shifts = keep["shifts"].rearrange("(n p) (t q) -> n p t q", p=RC, q=P)
        with nc.Block() as block:
            @block.gpsimd
            def _(pool):
                nc.gpsimd.memset(Q[:], 0.0).then_inc(zeroed, 1)

            @block.scalar
            def _(act):
                for dst, src in ((fold[:], a["fold"]), (slopes[:], a["slopes"]), (side[:], a["side"]), (ident[:], a["ident"])):
                    act.dma_start(dst, src).then_inc(loaded, 16)

            @block.sync
            def _(sp):
                sp.wait_ge(zeroed, 1)
                load_stacks(sp, a, keep, 0, Q, K[0], stacks_in, shifted=False)

                def store(n):
                    sp.wait_ge(step, PER * (n + 1))
                    for p in range(RC):
                        sp.dma_start(shifts[bass.ds(n, 1), p, :, :], parts[:, p, :]).then_inc(shift_out, 16)

                with sp.Fori(0, BH - 1) as n:
                    store(n)
                    load_stacks(sp, a, keep, n + 1, Q, K[0], stacks_in, shifted=False)
                store(BH - 1)
                sp.wait_ge(shift_out, 16 * RC * BH + 16)

            @block.tensor
            def _(pe):
                pe.wait_ge(loaded, 64)
                with pe.Fori(0, BH) as n:
                    pe.wait_ge(stacks_in, (LOADS - 16) * (n + 1))
                    pe.wait_ge(k_turned, n + 1)
                    for qt in range(KT):
                        pe.wait_ge(topped, KT * n + qt + 1)
                        for bank in range(BPB):
                            stack = K[0 if bank <= qt // TT else 1]
                            mm = pe.matmul(SC[:, bank, :], Q[:, qt * P:(qt + 1) * P], stack[:, bank * TB:(bank + 1) * TB],
                                           start=True, stop=True)
                        mm.then_inc(scored, 1)
                    pe.wait_ge(topped, KT * (n + 1) + 1)
                    pe.transpose(T[0:KT, 0:P], top[:], ident[:]).then_inc(turned, 1)

            @block.vector
            def _(dve):
                v = nc.vector
                steps = Steps(dve, step, PER)
                dve.sem_inc(topped, 1)
                dve.sem_inc(shift_out, 16)
                dve.wait_ge(loaded, 64)
                with dve.Fori(0, BH) as n:
                    steps.begin(n)
                    dve.wait_ge(stacks_in, (LOADS - 16) * (n + 1))
                    v.tensor_scalar(K[1][:], K[0][:], side[:], None, ALU.mult).then_inc(k_turned, 1)
                    for qt in range(KT):
                        dve.wait_ge(scored, KT * n + qt + 1)
                        at = qt % TT * P
                        sc = SC[:, qt // TT, at:TB]
                        steps(v.scalar_tensor_tensor(out=sc, in0=fold[:, 0:TB - at], scalar=slopes[:, bass.ds(n % H, 1)],
                                                     in1=sc, op0=ALU.mult, op1=ALU.add))
                        v.tensor_reduce(top[:, qt:qt + 1], SC[:], AX.XY, ALU.max).then_inc(topped, 1)
                    dve.wait_ge(turned, n + 1)
                    dve.wait_ge(shift_out, 16 * RC * n + 16)
                    steps(v.tensor_scalar(neg[:], T[0:KT, 0:P], -1.0, None, ALU.mult))
                    steps(v.tensor_copy(parts[:, 0, :], neg[:]))
                    steps(v.tensor_tensor(neg[:], neg[:], parts[:, 0, :], ALU.subtract))
                    steps(v.tensor_copy(parts[:, 1, :], neg[:]))
                    steps(v.tensor_tensor(parts[:, 2, :], neg[:], parts[:, 1, :], ALU.subtract))
                    steps.end()


def output_stage(nc, a, keep, out_dram):
    x_all, gate_all = keep["x_all"], keep["gate_all"]
    with ExitStack() as ctx:
        r = Room(nc, ctx, "out", keep)
        w_o = r.sb("w_o", [P, DC, D])
        o = r.sb("o", [P, BPB, DC, TB])
        y = r.sb("y", [P, BPB, TT, D])
        Z = r.ps("Z", [P, 2, 2, TB])
        loaded = r.sem("loaded")
        block_in = [r.sem(f"block_in{n}") for n in range(BPB)]
        projected = r.sem("projected")
        done = r.sem("done")
        stored = [r.sem(f"stored{n}") for n in range(BPB)]
        step = r.sem("step")
        IN = 16 * DC
        heads = keep["heads"].rearrange("(n g r) q -> n g r q", g=BPB, r=VW)
        results = out_dram.rearrange("b s d -> (b s) d")
        with nc.Block() as block:
            @block.sync
            def _(sp):
                sp.dma_start(w_o[:], a["wT_out"].rearrange("(c p) n -> p c n", p=P)).then_inc(loaded, 16)
                with sp.Fori(0, B) as b:
                    for g in range(BPB):
                        j, u = b * BPB + g, g
                        sp.wait_ge(done, j + 1)
                        sem = block_in[u]
                        for c in range(DC):
                            sp.dma_start(o[:, u, c, :], heads[bass.ds(b * H + 8 * c, 8), g, 0:HD, :]).then_inc(sem, 16)

            @block.scalar
            def _(act):
                with act.Fori(0, B) as b:
                    for g in range(BPB):
                        j, u = b * BPB + g, g
                        act.wait_ge(done, j + 1 + BPB)
                        act.dma_start(results[bass.ds(j * TB, TB), :].rearrange("(t p) d -> p t d", p=P), y[:, u]).then_inc(stored[u], 16)
                for u in range(BPB):
                    act.wait_ge(stored[u], 16 * (B + 1))

            @block.tensor
            def _(pe):
                pe.wait_ge(loaded, 16)
                with pe.Fori(0, B) as b:
                    for g in range(BPB):
                        j, u = b * BPB + g, g
                        pe.wait_ge(block_in[u], IN * (b + 1))
                        pe.wait_ge(done, j + 3)
                        for t in range(TT):
                            for c in range(DC):
                                mm = pe.matmul(Z[:, u % 2, t // 2, t % 2 * D:(t % 2 + 1) * D], o[:, u, c, t * P:(t + 1) * P],
                                               w_o[:, c, :], start=(c == 0), stop=(c == DC - 1))
                        mm.then_inc(projected, 1)

            @block.vector
            def _(dve):
                v = nc.vector
                steps = Steps(dve, step, BPB)

                def finish(b, g):
                    j, u = b * BPB + g, g
                    dve.wait_ge(projected, j + 1)
                    dve.wait_ge(stored[u], 16 * b + 16)
                    yy = y[:, u]
                    steps(v.tensor_tensor(yy, Z[:, u % 2].rearrange("p a (b d) -> p (a b) d", d=D),
                                          gate_all[:, bass.ds(j * TT, TT), :], ALU.mult))
                    v.tensor_tensor(yy, yy, x_all[:, bass.ds(j * TT, TT), :], ALU.add).then_inc(done, 1)

                dve.sem_inc(done, BPB)
                for u in range(BPB):
                    dve.sem_inc(stored[u], 16)
                with dve.Fori(0, B) as b:
                    steps.begin(b)
                    for g in range(BPB):
                        finish(b, g)
                    steps.end()


def build(nc, a, out):
    with ExitStack() as ctx:
        scratch = lambda name, shape, dt: nc.dram_tensor(name, shape, dt).ap()
        keep = {
            "whole": ctx,
            "x_all": ctx.enter_context(nc.sbuf_tensor("x_all", [P, NBLK * TT, D], F32)),
            "gate_all": ctx.enter_context(nc.sbuf_tensor("gate_all", [P, NBLK * TT, D], F32)),
            "redo": ctx.enter_context(nc.sbuf_tensor("redo", [1, 1], I32)),
            "q_parts": scratch("q_parts", (BH * 3 * HD, S), BF16),
            "k_parts": scratch("k_parts", (BH * 3 * HD, S), BF16),
            "values": scratch("values", (BH * P, KT * HD), F32),
            "shifts": scratch("shifts", (BH * RC, S), BF16),
            "heads": scratch("heads", (BH * P, TB), F32),
            "recips": scratch("recips", (BH * BPB, TB), F32),
        }
        tokens_stage(nc, a, keep)
        attention_stage(nc, a, keep, "own")
        redo = nc.values_load(keep["redo"][0:1, 0:1], min_val=0, max_val=1)
        with nc.If(redo != 0):
            maximum_stage(nc, a, keep)
            attention_stage(nc, a, keep, "top")
        output_stage(nc, a, keep, out)


NAMES = {
    "x": "L0_attn_x", "b_qkv": "L0_attn_b_qkv", "b_out": "L0_attn_b_out",
    "correction_bias": "L0_ffn_correction_bias", "w_gate": "L0_ffn_w_gate", "w_up": "L0_ffn_w_up",
    "w_down": "L0_ffn_w_down", "sw_gate": "L0_ffn_sw_gate", "sw_up": "L0_ffn_sw_up", "sw_down": "L0_ffn_sw_down",
}
TURNED = {"wT_qkv": "L0_attn_W_qkv", "wT_out": "L0_attn_W_out", "wT_router": "L0_ffn_router_weight"}


def kernel(**inputs):
    import concourse.bacc as bacc
    from concourse.bass_utils import run_bass_kernel_spmd

    nc = bacc.Bacc("TRN2", target_bir_lowering=False, num_devices=1)
    arrays = {k: np.ascontiguousarray(inputs[n]) for k, n in NAMES.items()}
    arrays |= {k: np.ascontiguousarray(np.transpose(inputs[n])) for k, n in TURNED.items()}
    arrays |= {k: np.ascontiguousarray(c) for k, c in constants().items()}
    a = {k: nc.dram_tensor(f"in_{k}", v.shape, mybir.dt.from_np(v.dtype), kind="ExternalInput").ap()
         for k, v in arrays.items()}
    out = nc.dram_tensor("out", (B, S, D), F32, kind="ExternalOutput").ap()
    build(nc, a, out)
    result = run_bass_kernel_spmd(nc, [{f"in_{k}": v for k, v in arrays.items()}], core_ids=[0])
    return result.results[0]["out"]
```
